# Optimizing a Trainium2 kernel written in Bass

```python
import numpy as np
import jax
import jax.numpy as jnp

def _softmax(x, axis=-1):
    return jax.nn.softmax(x, axis=axis)

def _gelu(x):
    return jax.nn.gelu(x, approximate=True)

def _silu(x):
    return jax.nn.silu(x)

def _sigmoid(x):
    return jax.nn.sigmoid(x)

def _layernorm(x, axis=-1, eps=1e-05):
    m = jnp.mean(x, axis=axis, keepdims=True)
    v = jnp.var(x, axis=axis, keepdims=True)
    return (x - m) / jnp.sqrt(v + eps)

def _scatter_add(tgt, idx, src, axis=0):
    return tgt.at[idx].add(src)

def _segment_sum(src, seg, n):
    return jax.ops.segment_sum(src, seg, n)
kernel_name = 'mk_adj_preln_d1_adj_r2_208341'

def setup_inputs(seed: int=0):
    np.random.seed(seed)
    _w = jnp.asarray

    def _rec_inputs():
        import jax
        import jax.numpy as jnp
        _gk = jax.random.key(seed)
        x = -0.003407 + 1.001 * jax.random.normal(jax.random.fold_in(_gk, 1), (8, 1024, 64), jnp.float32)
        _a = jax.random.bernoulli(jax.random.fold_in(_gk, 2), 0.00195312, (8, 1024, 1024))
        _a = jnp.logical_or(_a, jnp.swapaxes(_a, -1, -2))
        _af = _a.astype(jnp.float32)
        adj = _af
        _nm = jnp.ones((8, 1024), dtype=bool)
        nodemask = _nm
        return (x, adj, nodemask)
    x, adj, nodemask = _rec_inputs()

    def _L0_gnn_setup():
        import jax, jax.numpy as jnp
        import numpy as np
        TAUS = [0.25, 0.5, 0.75]
        QWEIGHTS = [0.25, 0.5, 0.25]
        T_THRESH = 10
        K_DIL = 2
        EPS_GIN = 0.0

        def _dilate_adj(adj, mask):
            B, N, _ = adj.shape
            eye = jnp.eye(N, dtype=bool)
            adj_ = jnp.where(eye[None], 1.0, adj)
            nb = (adj_ > 0) & (~eye)[None]
            m = nb.sum(-1)
            rank = jnp.cumsum(nb, axis=-1) - 1
            skip = jnp.where(m > T_THRESH, (m + K_DIL - 1) // K_DIL, 1)
            do_dil = (skip > 1) & mask
            removed = nb & do_dil[..., None] & ((rank + 1) % skip[..., None] == 0)
            rem = removed | jnp.swapaxes(removed, 1, 2)
            return jnp.where(rem, 0.0, adj_)

        def _weighted_nanquantile_agg(x, valid):
            B, N, C = x.shape
            big = jnp.finfo(x.dtype).max / 4
            vals = jnp.where(valid[..., None], x[:, None, :, :], big)
            sv = jnp.sort(vals, axis=2)
            m = valid.sum(-1)
            mf = m.astype(x.dtype)

            def gather(idx):
                idxb = jnp.broadcast_to(idx[:, :, None, None], (B, N, 1, C))
                return jnp.take_along_axis(sv, idxb, axis=2)[:, :, 0, :]
            agg = jnp.zeros_like(x)
            for tau, wt in zip(TAUS, QWEIGHTS):
                pos = jnp.clip(tau * (mf - 1.0), 0.0)
                lo = jnp.floor(pos).astype(jnp.int32)
                hi = jnp.ceil(pos).astype(jnp.int32)
                frac = (pos - lo.astype(x.dtype))[..., None]
                q = gather(lo) * (1.0 - frac) + gather(hi) * frac
                agg = agg + wt * q
            return jnp.where((m > 0)[..., None], agg, 0.0)
        key = jax.random.key(seed)
        k0, k1, k2, k3 = jax.random.split(key, 4)
        B, N, C, H, CO = (4, 256, 64, 128, 64)
        x = jax.random.normal(k0, (B, N, C), dtype=jnp.float32)
        u = jax.random.uniform(k1, (B, N, N))
        a = (u < 0.03).astype(jnp.float32)
        adj = jnp.maximum(a, jnp.swapaxes(a, 1, 2))
        mask = jnp.broadcast_to(jnp.arange(N) < N - 32, (B, N))
        W1 = jax.random.normal(k2, (C, H), dtype=jnp.float32) * (1.0 / np.sqrt(C))
        b1 = jnp.zeros((H,), dtype=jnp.float32)
        W2 = jax.random.normal(k3, (H, CO), dtype=jnp.float32) * (1.0 / np.sqrt(H))
        b2 = jnp.zeros((CO,), dtype=jnp.float32)
        return {'x': x, 'adj': adj, 'mask': mask, 'W1': W1, 'b1': b1, 'W2': W2, 'b2': b2}
    _L0_gnn_all = _L0_gnn_setup()
    _L0_gnn_in = {k: v for k, v in _L0_gnn_all.items() if k in ('W1', 'b1', 'W2', 'b2')}
    del _L0_gnn_all
    return {'x': x, 'adj': adj, 'nodemask': nodemask, 'L0_gnn_W1': _L0_gnn_in['W1'], 'L0_gnn_b1': _L0_gnn_in['b1'], 'L0_gnn_W2': _L0_gnn_in['W2'], 'L0_gnn_b2': _L0_gnn_in['b2']}

def reference(x, adj, nodemask, L0_gnn_W1, L0_gnn_b1, L0_gnn_W2, L0_gnn_b2):
    import jax
    import jax.numpy as jnp

    def _L0_gnn_ref(x, adj, mask, W1, b1, W2, b2):
        import jax, jax.numpy as jnp
        import numpy as np
        TAUS = [0.25, 0.5, 0.75]
        QWEIGHTS = [0.25, 0.5, 0.25]
        T_THRESH = 10
        K_DIL = 2
        EPS_GIN = 0.0

        def _dilate_adj(adj, mask):
            B, N, _ = adj.shape
            eye = jnp.eye(N, dtype=bool)
            adj_ = jnp.where(eye[None], 1.0, adj)
            nb = (adj_ > 0) & (~eye)[None]
            m = nb.sum(-1)
            rank = jnp.cumsum(nb, axis=-1) - 1
            skip = jnp.where(m > T_THRESH, (m + K_DIL - 1) // K_DIL, 1)
            do_dil = (skip > 1) & mask
            removed = nb & do_dil[..., None] & ((rank + 1) % skip[..., None] == 0)
            rem = removed | jnp.swapaxes(removed, 1, 2)
            return jnp.where(rem, 0.0, adj_)

        def _weighted_nanquantile_agg(x, valid):
            B, N, C = x.shape
            big = jnp.finfo(x.dtype).max / 4
            vals = jnp.where(valid[..., None], x[:, None, :, :], big)
            sv = jnp.sort(vals, axis=2)
            m = valid.sum(-1)
            mf = m.astype(x.dtype)

            def gather(idx):
                idxb = jnp.broadcast_to(idx[:, :, None, None], (B, N, 1, C))
                return jnp.take_along_axis(sv, idxb, axis=2)[:, :, 0, :]
            agg = jnp.zeros_like(x)
            for tau, wt in zip(TAUS, QWEIGHTS):
                pos = jnp.clip(tau * (mf - 1.0), 0.0)
                lo = jnp.floor(pos).astype(jnp.int32)
                hi = jnp.ceil(pos).astype(jnp.int32)
                frac = (pos - lo.astype(x.dtype))[..., None]
                q = gather(lo) * (1.0 - frac) + gather(hi) * frac
                agg = agg + wt * q
            return jnp.where((m > 0)[..., None], agg, 0.0)
        dtp = x.dtype
        adj_d = _dilate_adj(adj, mask)
        agg = _weighted_nanquantile_agg(x, adj_d > 0)
        out = (1.0 + EPS_GIN) * x + agg
        h = jax.nn.relu(jnp.einsum('bnc,ch->bnh', out, W1) + b1)
        y = jnp.einsum('bnh,ho->bno', h, W2) + b2
        return y * mask[..., None].astype(dtp)
    h = jnp.maximum(_layernorm(x, axis=-1), 0.0)
    x = x + _L0_gnn_ref(h, adj, nodemask, L0_gnn_W1, L0_gnn_b1, L0_gnn_W2, L0_gnn_b2)
    return x

_drawn_inputs = setup_inputs


def setup_inputs(seed=0):
    import zlib

    import numpy as np

    out = dict(_drawn_inputs(seed))
    spreads = {'L0_gnn_b1': (0.0, 0.1), 'L0_gnn_b2': (0.0, 0.1)}
    factors = {}
    for name, (base, spread) in spreads.items():
        noise = np.random.default_rng([zlib.crc32(name.encode()), seed]).standard_normal(out[name].shape)
        drawn = base * np.exp(spread * noise) if base else spread * noise
        out[name] = jnp.asarray(drawn.astype(out[name].dtype))
    for name, factor in factors.items():
        out[name] = (out[name] * factor).astype(out[name].dtype)
    return out
```

```python
import concourse.bass as bass
from concourse import mybir
from contextlib import ExitStack

FP32 = mybir.dt.float32
FP16 = mybir.dt.float16
BF16 = mybir.dt.bfloat16
I32 = mybir.dt.int32
ALU = mybir.AluOpType
ACT = mybir.ActivationFunctionType
AX = mybir.AxisListType

NETWORKS = {
    8: [(0, 2), (1, 3), (4, 6), (5, 7), (0, 4), (1, 5), (2, 6), (3, 7), (0, 1), (2, 3), (4, 5), (6, 7),
        (2, 4), (3, 5), (1, 4), (3, 6), (1, 2), (3, 4), (5, 6)],
    10: [(0, 8), (1, 9), (2, 7), (3, 5), (4, 6), (0, 2), (1, 4), (5, 8), (7, 9), (0, 3), (2, 4), (5, 7),
         (6, 9), (0, 1), (3, 6), (8, 9), (1, 5), (2, 3), (4, 8), (6, 7), (1, 2), (3, 5), (4, 6), (7, 8),
         (2, 3), (4, 5), (6, 7), (3, 4), (5, 6)],
    12: [(0, 8), (1, 7), (2, 6), (3, 11), (4, 10), (5, 9), (0, 1), (2, 5), (3, 4), (6, 9), (7, 8), (10, 11),
         (0, 2), (1, 6), (5, 10), (9, 11), (0, 3), (1, 2), (4, 6), (5, 7), (8, 11), (9, 10), (1, 4), (3, 5),
         (6, 8), (7, 10), (1, 3), (2, 5), (6, 9), (8, 10), (2, 3), (4, 5), (6, 7), (8, 9), (4, 6), (5, 7),
         (3, 4), (5, 6), (7, 8)],
}


def odd_even_merge(n):
    net, p = [], 1
    while p < n:
        k = p
        while k >= 1:
            for j in range(k % p, n - k, 2 * k):
                for i in range(min(k, n - j - k)):
                    if (i + j) // (2 * p) == (i + j + k) // (2 * p):
                        net.append((i + j, i + j + k))
            k //= 2
        p *= 2
    return net


NETWORKS[17] = odd_even_merge(17)


def top_rank(slots):
    return -(-3 * (slots - 1) // 4)


def network_steps(slots, spares):
    wanted = set(range(top_rank(slots) + 1))
    kept = []
    for a, b in reversed(NETWORKS[slots]):
        if a in wanted or b in wanted:
            kept.append((a, b, a in wanted, b in wanted))
            wanted |= {a, b}
    kept.reverse()
    at = list(range(slots))
    free = list(range(slots, slots + spares))
    layers = []
    while kept:
        layer, busy, freed, later = [], set(), [], []
        for a, b, low, high in kept:
            if a in busy or b in busy or not free:
                later.append((a, b, low, high))
                busy |= {a, b}
                continue
            busy |= {a, b}
            mn = free.pop(0) if low else None
            layer.append((at[a], at[b], mn, at[b] if high else None))
            if low:
                freed.append(at[a])
                at[a] = mn
        free += freed
        kept = later
        layers.append(layer)
    return layers, at


def quantile_gnn(nc, x, adj, nodemask, W1, b1, W2, b2, out):
    B, N, C = x.shape
    H = W1.shape[1]
    P = 128
    T = N // P
    NT = B * T
    BIG = 1e30
    PAD = B * N
    LIST = 16
    KM = 8
    R_ID, R_CNT, R_KEY, R_MASK = LIST, LIST + 1, LIST + 2, LIST + 3
    R_X = LIST + 4
    R_H = R_X + C
    R_REM = R_H + C
    RW = R_REM
    TW = C + 4
    REC = RW + 4
    TAUS = [(0.25, 0.25), (0.5, 0.5), (0.75, 0.25)]
    CLASSES = [(5, 10, 6), (2, 12, 3), (0, 17, 2)]
    NOV = 11
    CH = 2
    NRING = 6
    NCH = NT // CH
    AHEAD = 3
    NREC = AHEAD + 1

    MSP, OSP = 4, 3
    groups = [(KM, T, None)] * B + [(k, n, q0) for q0, k, n in CLASSES]
    MG = B
    PICK = MG - 1 - AHEAD - 1

    x_t = x.rearrange("b (t p) c -> p (b t) c", p=P)
    out_t = out.rearrange("b (t p) c -> p (b t) c", p=P)
    out_rows = out.rearrange("b n c -> (b n) c")
    adj_t = adj.rearrange("b (t p) j -> p (b t) j", p=P)
    tables = [nc.dram_tensor(f"table{b}", [N + 1, TW], FP32, kind="Internal").ap() for b in range(B)]
    table = nc.dram_tensor("table", [PAD + 1, TW], FP32, kind="Internal").ap()
    records = nc.dram_tensor("records", [PAD + 1, RW], FP32, kind="Internal").ap()
    table_t = table[0:PAD, :].rearrange("(t p) w -> p t w", p=P)
    h_turned = nc.dram_tensor("h_turned", [B, C, N], FP32, kind="Internal").ap()
    records_t = records[0:PAD, :].rearrange("(t p) w -> p t w", p=P)

    ctx = ExitStack()
    with ctx:
        def sb(name, shape, dt):
            return ctx.enter_context(nc.sbuf_tensor(name, shape, dt))

        def pb(name, shape):
            return ctx.enter_context(nc.psum_tensor(name, shape, FP32))

        def sem(name):
            return ctx.enter_context(nc.semaphore(name))

        x_all = sb("x_all", [P, NT, C], FP32)
        keyt = sb("keyt", [P, T, N], FP16)
        adj_ring = sb("adj_ring", [P, NRING, CH, N], FP32)
        keyed = sb("keyed", [P, 2, N], FP16)
        keyed2 = sb("keyed2", [P, 2, N], FP16)
        lists = sb("lists", [P, T, LIST], FP32)
        tmpa = sb("tmpa", [P, T, LIST], FP32)
        tmpb = sb("tmpb", [P, T, LIST], FP32)
        tmpc = sb("tmpc", [P, T, LIST], FP32)
        st = sb("st", [P, 5, T], FP32)
        less_mean = sb("less_mean", [P, NT], FP32)
        var = sb("var", [P, NT], FP32)
        xc = sb("xc", [P, T, C], FP32)
        rec = sb("rec", [P, NREC, T, REC], FP32)
        nidx = sb("nidx", [P, NREC, T, KM - 1], I32)
        key_sum = sb("key_sum", [P, NT], FP32)
        degree = sb("degree", [P, NT], FP32)
        gat = sb("gat", [P, 2, KM + MSP, T, TW], FP32)
        wsort = sb("wsort", [P, max(n * (top_rank(k) + 1) for k, n, _ in groups), C], FP32)
        wgt = sb("wgt", [P, 2, T, LIST], FP32)
        fl = sb("fl", [P, 3, max((k - 1) * n for k, n, _ in groups)], FP32)
        s2 = sb("s2", [P, 4, T], FP32)
        wt = sb("wt", [P, 2, T, LIST], FP32)
        oT = sb("oT", [C, T * P], FP32)
        h1 = sb("h1", [H, T * P], FP32)
        fin = sb("fin", [P, 2, T, C], FP32)
        fin2 = sb("fin2", [P, T, C], FP32)
        ident = sb("ident", [P, P], FP32)
        w1s = sb("w1s", [C, H], FP32)
        b1s = sb("b1s", [H, 1], FP32)
        w2s = sb("w2s", [H, C], FP32)
        b2s = sb("b2s", [1, C], FP32)
        ones1 = sb("ones1", [1, P], FP32)
        mask8 = sb("mask8", [NT, P], mybir.dt.uint8)
        maskr = sb("maskr", [NT, P], FP32)
        mask = sb("mask", [P, NT], FP32)
        kk = sb("kk", [P, LIST], FP32)
        kpos = sb("kpos", [P, LIST], FP32)
        gid = sb("gid", [P, NT], FP32)
        ownkey = sb("ownkey", [P, T], FP32)
        padrow = sb("padrow", [1, TW], FP32)
        padrec = sb("padrec", [1, RW], FP32)
        crow = sb("crow", [P, 3, NT], FP32)
        crowk = sb("crowk", [P, 16], FP32)
        crowi = sb("crowi", [P, 16], I32)
        crowf = sb("crowf", [P, 16], FP32)
        rid = sb("rid", [P, NOV], I32)
        rv = sb("rv", [P, NOV, RW], FP32)
        rvi = sb("rvi", [P, NOV, LIST + 1], I32)

        keyrow = wsort[:, :, :].rearrange("p a c -> p (a c)")[:, 0:N // 2].bitcast(FP16)
        adj_flat = adj_ring[:, :, :, :].rearrange("p a b n -> p (a b n)")
        ov_gat, at = [], 0
        for q0, k, n in CLASSES:
            size = (k + OSP) * n * TW
            ov_gat.append(adj_flat[:, at:at + size].rearrange("p (s t w) -> p s t w", s=k + OSP, t=n))
            at += size
        assert at <= NRING * CH * N

        def ring_part(k, dt, words):
            part = adj_flat[:, k:k + words]
            return part if dt == FP32 else part.bitcast(dt)

        g_adj = ring_part(0, FP32, N)
        g_scan = ring_part(N, FP32, N)
        g_tmp = ring_part(2 * N, FP32, N)
        g_row = ring_part(3 * N, FP32, N)
        g_valid = ring_part(4 * N, BF16, T * N // 2).rearrange("p (t n) -> p t n", t=T)
        g_ones = ring_part(8 * N, BF16, N // 2)
        g_flip = ring_part(9 * N, BF16, N // 2)
        g_ident = ring_part(10 * N, BF16, P // 2)
        g_small = ring_part(11 * N, FP32, 512)
        gat_flat = gat[:, :, :, :, :].rearrange("p a s t w -> p (a s t w)")
        g_gone = gat_flat[:, 0:T * N // 2].bitcast(BF16).rearrange("p (t n) -> p t n", t=T)
        g_less = g_gone
        g_turned = gat_flat[:, T * N // 2:T * N].bitcast(BF16).rearrange("p (t n) -> p t n", t=T)
        g_h = gat_flat[:, T * N:T * N + T * C].rearrange("p (t c) -> p t c", t=T)
        g_agg = gat_flat[:, T * N + T * C:T * N + 2 * T * C].rearrange("p (t c) -> p t c", t=T)

        oT_full = pb("oT_full", [P, T * P])
        oT_ps = oT_full[0:C, :]
        h1_ps = pb("h1_ps", [H, T * P])
        y_ps = pb("y_ps", [P, T, C])
        m_ps = pb("m_ps", [P, 512])
        flip_ps = ctx.enter_context(nc.psum_tensor("flip_ps", [P, N], BF16))
        crowd_flag = sb("crowd_flag", [P, 4], FP32)
        general = sb("general", [1, 1], I32)

        def slots_of(g):
            return gat[:, g % 2, :, :, :] if g < MG else ov_gat[g - MG]

        def rec_of(g, a, z):
            if g < MG:
                return rec[:, g % NREC, :, a:z]
            k, n, q0 = groups[g]
            return rv[:, q0:q0 + n, a:z]

        x_in = sem("x_in")
        small_in = sem("small_in")
        adj_in = [sem(f"adj_in{i}") for i in range(NRING)]
        tile_listed = sem("tile_listed")
        consts_made = sem("consts_made")
        pool_step = sem("pool_step")
        dve_step = sem("dve_step")
        pads_made = sem("pads_made")
        pads_out = sem("pads_out")
        mask_float = sem("mask_float")
        mask_turned = sem("mask_turned")
        var_ready = sem("var_ready")
        std_ready = sem("std_ready")
        records_ready = sem("records_ready")
        stored = [sem(f"stored{i}") for i in range(NREC)]
        self_in = sem("self_in")
        gathered = [sem(f"gathered{i}") for i in range(2)] + [sem(f"gathered_ov{i}") for i in range(len(CLASSES))]
        crowd_ready = sem("crowd_ready")
        recs_gathered = sem("recs_gathered")
        crowd_idx = sem("crowd_idx")
        sorted_ready = sem("sorted_ready")
        weighted = sem("weighted")
        summed = sem("summed")
        sum_out = sem("sum_out")
        hidden = sem("hidden")
        hidden_out = sem("hidden_out")
        y_ready = sem("y_ready")
        fin_ready = sem("fin_ready")
        out_done = [sem(f"out_done{i}") for i in range(2)]
        scattered = [sem(f"scattered{i}") for i in range(len(CLASSES))]

        flag_part = sem("flag_part")
        flag_sum = sem("flag_sum")
        flag_ready = sem("flag_ready")
        all_stored = sem("all_stored")
        g_const = sem("g_const")
        g_adj_in = sem("g_adj_in")
        g_adj_used = sem("g_adj_used")
        g_gone_ready = sem("g_gone_ready")
        g_flip_ready = sem("g_flip_ready")
        g_flip_used = sem("g_flip_used")
        g_valid_ready = sem("g_valid_ready")
        g_turn_ready = sem("g_turn_ready")
        g_turn_out = sem("g_turn_out")
        g_h_in = sem("g_h_in")
        g_hT_ready = sem("g_hT_ready")
        g_hT_out = sem("g_hT_out")
        g_hT_stored = sem("g_hT_stored")
        g_row_in = sem("g_row_in")
        g_less_ready = sem("g_less_ready")
        g_count_ready = sem("g_count_ready")
        g_count_used = sem("g_count_used")
        g_chan_done = sem("g_chan_done")
        g_agg_ready = sem("g_agg_ready")
        g_sum_ready = sem("g_sum_ready")
        g_sum_out = sem("g_sum_out")
        g_hid_ready = sem("g_hid_ready")
        g_hid_out = sem("g_hid_out")
        g_y_ready = sem("g_y_ready")
        g_fin_ready = sem("g_fin_ready")
        g_out_done = sem("g_out_done")
        g_passed = sem("g_passed")

        block = ctx.enter_context(nc.Block())

        def general_taken(eng):
            eng.wait_ge(flag_ready, 1)
            return eng.value_load(general[0:1, 0:1], min_val=0, max_val=1)

        @block.sync
        def _(sp):
            sp.dma_start(x_all[:, 0:T, :], x_t[:, 0:T, :]).then_inc(x_in, 16)
            for c in range(2):
                sp.dma_start(adj_ring[:, c, :, :], adj_t[:, c * CH:(c + 1) * CH, :]).then_inc(adj_in[c], 16)
            sp.dma_start(mask8[:, :], nodemask.rearrange("b (t p) -> (b t) p", p=P)).then_inc(small_in, 16)
            sp.dma_start(w1s[:, :], W1).then_inc(small_in, 16)
            sp.dma_start(b1s[:, :], b1.rearrange("(h a) -> h a", a=1)).then_inc(small_in, 16)
            sp.dma_start(w2s[:, :], W2).then_inc(small_in, 16)
            sp.dma_start(b2s[:, :], b2.rearrange("(a c) -> a c", a=1)).then_inc(small_in, 16)
            for c in range(2, NCH):
                if c == 3:
                    sp.wait_ge(x_in, 16)
                    sp.dma_start(x_all[:, T:NT, :], x_t[:, T:NT, :]).then_inc(x_in, 16)
                if c >= NRING:
                    sp.wait_ge(tile_listed, (c - NRING + 1) * CH)
                sp.dma_start(adj_ring[:, c % NRING, :, :],
                             adj_t[:, c * CH:(c + 1) * CH, :]).then_inc(adj_in[c % NRING], 16)

            with sp.If(general_taken(sp) > 0):
                sp.wait_ge(all_stored, 1)
                with sp.Fori(0, B) as b:
                    sp.dma_start(g_h, records_t[:, bass.ds(b * T, T), R_H:R_H + C]).then_inc(g_h_in, 16)
                    for i in range(T):
                        sp.wait_ge(g_adj_used, b * T + i + 1)
                        sp.dma_start(g_adj, adj_t[:, bass.ds(b * T + i, 1), :].rearrange(
                            "p t n -> p (t n)")).then_inc(g_adj_in, 16)
                    sp.wait_ge(g_hT_out, b + 1)
                    sp.dma_start(h_turned[bass.ds(b, 1), :, :].rearrange("b c n -> c (b n)"),
                                 oT[:, :]).then_inc(g_hT_stored, 16)
                    sp.wait_ge(g_hT_stored, 16 * (b + 1))
                    sp.sem_inc(g_passed, 1)
                    with sp.Fori(0, C) as c:
                        sp.wait_ge(g_chan_done, b * C + c + 1)
                        sp.dma_start(g_row, h_turned[bass.ds(b, 1), bass.ds(c, 1), :].rearrange(
                            "b c n -> (b c) n").partition_broadcast(P)).then_inc(g_row_in, 16)
                    sp.wait_ge(g_fin_ready, b + 1)
                    sp.dma_start(out_t[:, bass.ds(b * T, T), :], fin[:, 0, :, :]).then_inc(g_out_done, 16)
                    sp.wait_ge(g_out_done, 16 * (b + 1))
                    sp.sem_inc(g_passed, 1)

        @block.gpsimd
        def _(pool):
            pool.memset(ident[:, :], 0.0).then_inc(pool_step, 1)
            pool.iota(keyrow[:, :], [[-1, N]], base=N, channel_multiplier=0,
                      allow_small_or_imprecise_dtypes=True).then_inc(pool_step, 1)
            pool.wait_ge(pool_step, 2)
            for i in range(T):
                pool.affine_select(out=keyt[:, i, :], in_=keyrow[:, :], compare_op=ALU.not_equal, fill=0.0,
                                   base=i * P, pattern=[[-1, N]], channel_multiplier=1).then_inc(consts_made, 1)
            pool.iota(kk[:, :], [[1, LIST]], base=1, channel_multiplier=0,
                      allow_small_or_imprecise_dtypes=True)
            pool.iota(kpos[:, :], [[1, LIST]], base=0, channel_multiplier=0,
                      allow_small_or_imprecise_dtypes=True)
            pool.iota(gid[:, :], [[P, NT]], base=0, channel_multiplier=1,
                      allow_small_or_imprecise_dtypes=True)
            pool.iota(ownkey[:, :], [[-P, T]], base=N, channel_multiplier=-1,
                      allow_small_or_imprecise_dtypes=True)
            pool.memset(ones1[:, :], 1.0)
            pool.affine_select(out=ident[:, :], in_=ident[:, :], compare_op=ALU.not_equal, fill=1.0,
                               base=0, pattern=[[-1, P]], channel_multiplier=1).then_inc(consts_made, 1)

            def gather(g):
                k, n, q0 = groups[g]
                for i in range(n):
                    for s in range(k - 1):
                        idx = nidx[:, g % NREC, i, s:s + 1] if g < MG else rvi[:, q0 + i, s:s + 1]
                        pool.indirect_dma_start(
                            out=slots_of(g)[:, s, i, :], out_offset=None,
                            in_=tables[g][:, :] if g < MG else table[:, :],
                            in_offset=bass.IndirectOffsetOnAxis(ap=idx, axis=0),
                            bounds_check=N if g < MG else PAD, oob_is_err=False,
                        ).then_inc(gathered[g % 2 if g < MG else 2 + g - MG], 16)

            pool.wait_ge(pads_out, 16 * (B + 2))
            for g in range(MG):
                if g >= 2:
                    pool.wait_ge(weighted, g - 1)
                pool.wait_ge(stored[g % NREC], 48 * (g // NREC + 1))
                if g == MG - 1:
                    pool.wait_ge(crowd_ready, 1)
                    for i in range(NREC):
                        pool.wait_ge(stored[i], 48 * (MG // NREC))
                    for q in range(NOV):
                        pool.indirect_dma_start(
                            out=rv[:, q, :], out_offset=None, in_=records[:, :],
                            in_offset=bass.IndirectOffsetOnAxis(ap=rid[:, q:q + 1], axis=0),
                            bounds_check=PAD, oob_is_err=False).then_inc(recs_gathered, 16)
                gather(g)
            pool.wait_ge(crowd_idx, 1)
            for g in range(MG, len(groups)):
                gather(g)
            for i in range(2):
                pool.wait_ge(out_done[i], 16 * (MG // 2))
            for g in range(MG, len(groups)):
                k, n, q0 = groups[g]
                pool.wait_ge(fin_ready, g + 1)
                for i in range(n):
                    pool.indirect_dma_start(
                        out=out_rows, out_offset=bass.IndirectOffsetOnAxis(
                            ap=rvi[:, q0 + i, LIST:LIST + 1], axis=0),
                        in_=fin[:, g % 2, i, :], in_offset=None,
                        bounds_check=PAD - 1, oob_is_err=False).then_inc(scattered[g - MG], 16)
            for g in range(MG, len(groups)):
                pool.wait_ge(scattered[g - MG], 16 * groups[g][1])
            pool.engine_nop().then_inc(all_stored, 1)

        @block.vector
        def _(dve):
            count = {}

            def note(ins, s=None):
                s = dve_step if s is None else s
                count[id(s)] = count.get(id(s), 0) + 1
                ins.then_inc(s, 1)
                return s, count[id(s)]

            def step(ins, s=None):
                dve.wait_ge(*note(ins, s))

            def row(i):
                return st[:, i, :]

            def over(ap, shape):
                return ap.unsqueeze(2).to_broadcast(shape)

            def statistics(b0, b1):
                dve.wait_ge(x_in, 16 if b0 == 0 else 32)
                for b in range(b0, b1):
                    cut = slice(b * T, (b + 1) * T)
                    xb = x_all[:, cut, :]
                    step(nc.vector.tensor_reduce(less_mean[:, cut], xb, axis=AX.X, op=ALU.add))
                    step(nc.vector.tensor_scalar(less_mean[:, cut], less_mean[:, cut], -1.0 / C, None, ALU.mult))
                    step(nc.vector.tensor_tensor(xc[:, :, :], xb, over(less_mean[:, cut], [P, T, C]), ALU.add))
                    step(nc.vector.tensor_tensor(xc[:, :, :], xc[:, :, :], xc[:, :, :], ALU.mult))
                    step(nc.vector.tensor_reduce(var[:, cut], xc[:, :, :], axis=AX.X, op=ALU.add))
                cut = slice(b0 * T, b1 * T)
                note(nc.vector.tensor_scalar(var[:, cut], var[:, cut], 1.0 / C, 1e-5, ALU.mult, ALU.add), var_ready)

            def normalise(b):
                cut = slice(b * T, (b + 1) * T)
                xb = x_all[:, cut, :]
                if b < 2:
                    dve.wait_ge(std_ready, b + 1)
                    part = var[:, 0:T] if b == 0 else var[:, T:NT]
                    step(nc.vector.reciprocal(part, part))
                if b >= NREC:
                    dve.wait_ge(stored[b % NREC], 48 * (b // NREC))
                    dve.wait_ge(summed, b - NREC + 1)
                r = rec[:, b % NREC, :, :]
                step(nc.vector.tensor_tensor(xc[:, :, :], xb, over(less_mean[:, cut], [P, T, C]), ALU.add))
                step(nc.vector.tensor_tensor(xc[:, :, :], xc[:, :, :], over(var[:, cut], [P, T, C]), ALU.mult))
                note(nc.vector.tensor_scalar(r[:, :, R_H:R_H + C], xc[:, :, :], 0.0, None, ALU.max))
                note(nc.vector.tensor_copy(r[:, :, R_X:R_X + C], xb))
                note(nc.vector.memset(r[:, :, R_REM + 2:R_REM + 4], 0.0))

            def list_rows(b):
                for i in range(T):
                    t = b * T + i
                    c = t // CH
                    if t % CH == 0:
                        dve.wait_ge(adj_in[c % NRING], 16 * (c // NRING + 1))
                    if b == 0:
                        dve.wait_ge(consts_made, i + 1)
                    step(nc.vector.scalar_tensor_tensor(
                        keyed[:, t % 2, :], adj_ring[:, c % NRING, t % CH, :], 0.0, keyt[:, i, :],
                        ALU.is_gt, ALU.mult, accum_out=key_sum[:, t:t + 1]), tile_listed)
                    step(nc.vector.max(lists[:, i, 0:8], keyed[:, t % 2, :]))
                    step(nc.vector.match_replace(keyed2[:, t % 2, :], lists[:, i, 0:8], keyed[:, t % 2, :], 0.0))
                    last = note(nc.vector.max(lists[:, i, 8:16], keyed2[:, t % 2, :]))
                dve.wait_ge(*last)

            def dilate(b):
                r = rec[:, b % NREC, :, :]
                deg = degree[:, b * T:(b + 1) * T]
                L, full = lists[:, :, :], [P, T, LIST]
                if b == 0:
                    dve.wait_ge(consts_made, T + 1)
                    dve.wait_ge(mask_turned, 1)
                    step(nc.vector.tensor_copy(mask[:, :], m_ps[:, 0:NT]))
                step(nc.vector.tensor_scalar(tmpa[:, :, :], L, 0.0, None, ALU.is_gt))
                step(nc.vector.tensor_reduce(deg, tmpa[:, :, :], axis=AX.X, op=ALU.add))
                cut = slice(b * T, (b + 1) * T)
                step(nc.vector.tensor_reduce(row(0), L, axis=AX.X, op=ALU.add))
                note(nc.vector.tensor_tensor(key_sum[:, cut], key_sum[:, cut], row(0), ALU.subtract))
                step(nc.vector.tensor_scalar(row(3), deg, 11.0, 6.0, ALU.is_ge, ALU.mult))
                step(nc.vector.scalar_tensor_tensor(row(3), deg, 13.0, row(3), ALU.is_ge, ALU.add))
                step(nc.vector.scalar_tensor_tensor(row(3), deg, 15.0, row(3), ALU.is_ge, ALU.add))
                step(nc.vector.tensor_tensor(row(3), row(3), mask[:, b * T:(b + 1) * T], ALU.mult))
                step(nc.vector.tensor_scalar(row(4), row(3), 2.0, None, ALU.mult))
                places = kk[:, :].unsqueeze(1).to_broadcast(full)
                for n, place in enumerate((row(3), row(4))):
                    step(nc.vector.tensor_tensor(tmpa[:, :, :], places, over(place, full), ALU.is_equal))
                    step(nc.vector.tensor_tensor(tmpb[:, :, :], tmpa[:, :, :], L, ALU.mult))
                    note(nc.vector.tensor_reduce(r[:, :, R_REM + n:R_REM + n + 1], tmpb[:, :, :], axis=AX.X,
                                                 op=ALU.add))
                    step(nc.vector.tensor_tensor(L, L, tmpb[:, :, :], ALU.subtract))
                step(nc.vector.tensor_scalar(tmpa[:, :, :], L, 0.0, None, ALU.is_gt))
                note(nc.vector.tensor_reduce(r[:, :, R_CNT:R_CNT + 1], tmpa[:, :, :], axis=AX.X, op=ALU.add))
                if b >= NREC:
                    dve.wait_ge(gathered[b % 2], 16 * T * (KM - 1) * ((b - NREC) // 2 + 1))
                note(nc.vector.tensor_scalar(nidx[:, b % NREC, :, :], lists[:, :, 0:KM - 1], -1.0, float(N),
                                             ALU.mult, ALU.add))
                step(nc.vector.tensor_scalar(tmpb[:, :, :], tmpa[:, :, :], float(b * N + N - PAD), None,
                                             ALU.mult))
                step(nc.vector.scalar_tensor_tensor(tmpc[:, :, :], L, -1.0, tmpb[:, :, :], ALU.mult, ALU.add))
                step(nc.vector.tensor_scalar(r[:, :, 0:LIST], tmpc[:, :, :], float(PAD), None, ALU.add))
                note(nc.vector.tensor_copy(r[:, :, R_ID], gid[:, b * T:(b + 1) * T]))
                note(nc.vector.tensor_copy(r[:, :, R_KEY], ownkey[:, :]))
                note(nc.vector.tensor_copy(r[:, :, R_MASK], mask[:, b * T:(b + 1) * T]), records_ready)

            def pick_crowded():
                k1, k2 = crow[:, 0, :], crow[:, 1, :]
                step(nc.vector.tensor_scalar(k1, degree[:, :], 1.0, float(NT), ALU.add, ALU.mult))
                step(nc.vector.tensor_tensor(k1, k1, tpos, ALU.add))
                step(nc.vector.scalar_tensor_tensor(k1, degree[:, :], float(KM - 1), k1, ALU.is_gt, ALU.mult))
                step(nc.vector.max(crowk[:, 0:8], k1))
                step(nc.vector.match_replace(k2, crowk[:, 0:8], k1, 0.0))
                step(nc.vector.max(crowk[:, 8:16], k2))
                step(nc.vector.tensor_copy(crowi[:, :], crowk[:, :]))
                step(nc.vector.tensor_scalar(crowi[:, :], crowi[:, :], NT - 1, None, ALU.bitwise_and))
                step(nc.vector.tensor_copy(crowf[:, :], crowi[:, :]))
                step(nc.vector.tensor_scalar(crowf[:, :], crowf[:, :], float(P), gid[:, 0:1], ALU.mult, ALU.add))
                step(nc.vector.tensor_scalar(crowf[:, :], crowf[:, :], float(-PAD), None, ALU.add))
                step(nc.vector.scalar_tensor_tensor(crowf[:, :], crowk[:, :], 0.0, crowf[:, :],
                                                    ALU.is_gt, ALU.mult))
                note(nc.vector.tensor_scalar(rid[:, :], crowf[:, 0:NOV], float(PAD), None, ALU.add), crowd_ready)

                f = crowd_flag
                step(nc.vector.tensor_reduce(f[:, 0:1], key_sum[:, :], axis=AX.X, op=ALU.max))
                step(nc.vector.tensor_scalar(f[:, 0:1], f[:, 0:1], 0.0, None, ALU.is_gt))
                step(nc.vector.scalar_tensor_tensor(f[:, 0:1], crowk[:, NOV:NOV + 1], 0.0, f[:, 0:1],
                                                    ALU.is_gt, ALU.max))
                for q0, k, n in CLASSES:
                    step(nc.vector.scalar_tensor_tensor(f[:, 0:1], crowk[:, q0:q0 + 1], float((k + 1) * NT),
                                                        f[:, 0:1], ALU.is_ge, ALU.max))
                note(nc.vector.memset(f[:, 1:2], 1.0), flag_part)
                dve.wait_ge(flag_sum, 1)
                note(nc.vector.tensor_scalar(general[:, :], m_ps[0:1, 0:1], 0.0, None, ALU.is_gt), flag_ready)

            def general_path():
                dve.wait_ge(all_stored, 1)
                done = nc.vector.memset(g_ones, 1.0).then_inc(g_const, 1)
                dve.wait_ge(g_const, 1)
                nc.vector.tensor_copy(g_ident, ident[:, :]).then_inc(g_const, 1)
                dve.wait_ge(g_const, 2)
                g_k = g_small[:, 64:64 + 6 * T].rearrange("p (t s) -> p t s", t=T)
                g_w = g_small[:, 128:128 + 6 * T].rearrange("p (t s) -> p t s", t=T)
                g_ki = g_small[:, 192:192 + 3 * T].bitcast(I32).rearrange("p (q t) -> p q t", q=3)
                g_kj = g_small[:, 216:216 + 3 * T].bitcast(I32).rearrange("p (q t) -> p q t", q=3)
                g_kf = g_small[:, 240:240 + 3 * T].rearrange("p (q t) -> p q t", q=3)
                g_kg = g_small[:, 264:264 + 3 * T].rearrange("p (q t) -> p q t", q=3)
                g_skip = g_small[:, 288:289]
                g_skipi = g_small[:, 289:290].bitcast(I32)
                g_two = g_small[:, 290:291]
                g_do = g_small[:, 291:292]
                g_cnt = g_small[:, 296:296 + T]
                g_q = g_small[:, 304:310]
                g_q2 = g_small[:, 310:316]

                def sure(ins):
                    dve.drain()

                for free in (g_adj_used, g_chan_done, g_flip_used, g_turn_out):
                    dve.sem_inc(free, 1)
                with dve.Fori(0, B) as b:
                    for i in range(T):
                        dve.wait_ge(g_adj_in, 16 * (b * T + i + 1))
                        nb, gone = g_valid[:, i, :], g_gone[:, i, :]
                        sure(nc.vector.scalar_tensor_tensor(g_flip, g_adj, 0.0, keyt[:, i, :], ALU.is_gt, ALU.mult))
                        dve.sem_inc(g_adj_used, 1)
                        sure(nc.vector.tensor_scalar(nb, g_flip, 0.0, None, ALU.is_gt))
                        sure(nc.vector.tensor_tensor_scan(g_scan, g_ones, nb, 0.0, ALU.mult, ALU.add))
                        m = g_scan[:, N - 1:N]
                        sure(nc.vector.tensor_scalar(g_skipi, m, 1.0, None, ALU.add))
                        sure(nc.vector.tensor_scalar(g_skipi, g_skipi, 1, None, ALU.logical_shift_right))
                        sure(nc.vector.tensor_copy(g_skip, g_skipi))
                        sure(nc.vector.tensor_scalar(g_do, m, 10.0, None, ALU.is_gt))
                        sure(nc.vector.tensor_tensor(g_do, g_do, mask[:, bass.ds(b * T + i, 1)], ALU.mult))
                        sure(nc.vector.tensor_tensor(g_skip, g_skip, g_do, ALU.mult))
                        sure(nc.vector.tensor_scalar(g_two, g_skip, 2.0, None, ALU.mult))
                        sure(nc.vector.tensor_scalar(g_tmp, g_scan, g_skip, None, ALU.is_equal))
                        sure(nc.vector.scalar_tensor_tensor(g_tmp, g_scan, g_two, g_tmp, ALU.is_equal, ALU.add))
                        sure(nc.vector.tensor_tensor(gone, g_tmp, nb, ALU.mult))
                        sure(nc.vector.tensor_tensor(nb, nb, gone, ALU.subtract))
                    dve.sem_inc(g_gone_ready, 1)
                    for i in range(T):
                        v = g_valid[:, i, :]
                        dve.wait_ge(g_flip_ready, b * T + i + 1)
                        sure(nc.vector.tensor_scalar(g_flip, flip_ps[:, :], -1.0, 1.0, ALU.mult, ALU.add))
                        dve.sem_inc(g_flip_used, 1)
                        sure(nc.vector.tensor_tensor(v, v, g_flip, ALU.mult))
                        sure(nc.vector.scalar_tensor_tensor(v, keyt[:, i, :], 0.0, v, ALU.is_equal, ALU.add))
                        sure(nc.vector.tensor_reduce(g_cnt[:, i:i + 1], v, axis=AX.X, op=ALU.add))
                    dve.sem_inc(g_valid_ready, 1)
                    for q in range(3):
                        sure(nc.vector.tensor_scalar(g_ki[:, q, :], g_cnt, -1.0, float(q + 1), ALU.add, ALU.mult))
                    sure(nc.vector.tensor_scalar(g_kj, g_ki, 2, None, ALU.logical_shift_right))
                    sure(nc.vector.tensor_scalar(g_ki, g_ki, 3, None, ALU.bitwise_and))
                    sure(nc.vector.tensor_copy(g_kf, g_kj))
                    sure(nc.vector.tensor_copy(g_kg, g_ki))
                    for q, (tau, share) in enumerate(TAUS):
                        sure(nc.vector.tensor_copy(g_k[:, :, 2 * q], g_kf[:, q, :]))
                        sure(nc.vector.tensor_scalar(g_k[:, :, 2 * q + 1], g_kf[:, q, :], 1.0, None, ALU.add))
                        sure(nc.vector.tensor_scalar(g_w[:, :, 2 * q + 1], g_kg[:, q, :], share / 4, None, ALU.mult))
                        sure(nc.vector.tensor_scalar(g_w[:, :, 2 * q], g_kg[:, q, :], -share / 4, share,
                                                     ALU.mult, ALU.add))
                    for i in range(T):
                        dve.wait_ge(g_turn_ready, b * T + i + 1)
                        sure(nc.vector.tensor_copy(g_turned[:, i, :], flip_ps[:, :]))
                        dve.sem_inc(g_turn_out, 1)
                    dve.wait_ge(g_h_in, 16 * (b + 1))
                    dve.sem_inc(g_passed, 1)
                    with dve.Fori(0, C) as c:
                        dve.wait_ge(g_row_in, 16 * (b * C + c + 1))
                        for i in range(T):
                            nc.vector.tensor_scalar(g_less[:, i, :], g_row, g_h[:, i, bass.ds(c, 1)], None, ALU.is_gt)
                        dve.drain()
                        dve.sem_inc(g_less_ready, 1)
                        for i in range(T):
                            ps = (oT_full, h1_ps)[i % 2]
                            dve.wait_ge(g_count_ready, (b * C + c) * T + i + 1)
                            for q in range(6):
                                sure(nc.vector.scalar_tensor_tensor(g_tmp, ps[:, :], g_k[:, i, q:q + 1], g_row,
                                                                    ALU.is_le, ALU.mult))
                                sure(nc.vector.tensor_reduce(g_q[:, q:q + 1], g_tmp, axis=AX.X, op=ALU.max))
                            dve.sem_inc(g_count_used, 1)
                            sure(nc.vector.tensor_tensor(g_q2, g_q, g_w[:, i, :], ALU.mult))
                            sure(nc.vector.tensor_reduce(g_agg[:, i, bass.ds(c, 1)], g_q2, axis=AX.X, op=ALU.add))
                        dve.sem_inc(g_chan_done, 1)
                    dve.sem_inc(g_agg_ready, 1)
                    dve.wait_ge(g_y_ready, b + 1)
                    sure(nc.vector.tensor_tensor(fin2[:, :, :], y_ps[:, :, :], over(mask[:, bass.ds(b * T, T)], [P, T, C]),
                                                 ALU.mult))
                    sure(nc.vector.tensor_tensor(fin[:, 0, :, :], fin2[:, :, :], x_all[:, bass.ds(b * T, T), :], ALU.add))
                    dve.sem_inc(g_fin_ready, 1)

            def crowded_indices():
                dve.wait_ge(recs_gathered, 16 * NOV)
                note(nc.vector.tensor_copy(rvi[:, :, :], rv[:, :, 0:LIST + 1]), crowd_idx)

            def sort_group(g):
                k, n, q0 = groups[g]
                top = top_rank(k) + 1
                G = slots_of(g)
                if g < MG:
                    dve.wait_ge(gathered[g % 2], 16 * T * (KM - 1) * (g // 2 + 1))
                else:
                    dve.wait_ge(gathered[2 + g - MG], 16 * n * (k - 1))
                f = [fl[:, i, 0:(k - 1) * n].rearrange("p (s t) -> p s t", s=k - 1) for i in range(3)]
                own = rec_of(g, R_KEY, R_KEY + 1).rearrange("p t a -> p a t").to_broadcast([P, k - 1, n])
                note(nc.vector.tensor_tensor(f[0], G[:, 0:k - 1, :, C], own, ALU.is_equal))
                step(nc.vector.tensor_tensor(f[1], G[:, 0:k - 1, :, C + 1], own, ALU.is_equal))
                step(nc.vector.tensor_tensor(f[2], f[0], f[1], ALU.add))
                note(nc.vector.tensor_scalar(f[0], f[2], BIG, None, ALU.mult))
                step(nc.vector.tensor_reduce(s2[:, 0, 0:n], f[2].rearrange("p s t -> p t s"), axis=AX.X,
                                             op=ALU.add))
                step(nc.vector.tensor_tensor(s2[:, 1, 0:n], rec_of(g, R_CNT, R_CNT + 1).rearrange(
                    "p t a -> p (t a)"), s2[:, 0, 0:n], ALU.subtract))
                if g >= 2:
                    dve.wait_ge(weighted, g - 1)
                W, a, c, d = wgt[:, g % 2, 0:n, 0:top], wt[:, 0, 0:n, 0:top], wt[:, 1, 0:n, 0:top], [P, n, top]
                ranks = kpos[:, 0:top].unsqueeze(1).to_broadcast(d)
                for q, (tau, share) in enumerate(TAUS):
                    step(nc.vector.tensor_scalar(s2[:, 2, 0:n], s2[:, 1, 0:n], tau, None, ALU.mult))
                    step(nc.vector.tensor_tensor(a, ranks, over(s2[:, 2, 0:n], d), ALU.subtract))
                    step(nc.vector.tensor_scalar(c, a, -1.0, 1.0, ALU.mult, ALU.add))
                    step(nc.vector.scalar_tensor_tensor(a, a, 1.0, c, ALU.add, ALU.min))
                    if q == 0:
                        step(nc.vector.tensor_scalar(W, a, 0.0, share, ALU.max, ALU.mult))
                    else:
                        step(nc.vector.tensor_scalar(a, a, 0.0, share, ALU.max, ALU.mult))
                        step(nc.vector.tensor_tensor(W, W, a, ALU.add))
                dve.wait_ge(self_in, g + 1)
                for s in range(k - 1):
                    last = note(nc.vector.tensor_tensor(G[:, s, :, 0:C], G[:, s, :, 0:C],
                                                        over(f[0][:, s, :], [P, n, C]), ALU.max))
                layers, _ = network_steps(k, MSP if g < MG else OSP)
                for layer in layers:
                    dve.wait_ge(*last)
                    mins = []
                    for sa, sb_, mn, mx in layer:
                        if mn is not None:
                            mins.append(note(nc.vector.tensor_tensor(
                                G[:, mn, :, 0:C], G[:, sa, :, 0:C], G[:, sb_, :, 0:C], ALU.min)))
                            last = mins[-1]
                        else:
                            mins.append(None)
                    for (sa, sb_, mn, mx), read in zip(layer, mins):
                        if mx is not None:
                            if read:
                                dve.wait_ge(*read)
                            last = note(nc.vector.tensor_tensor(
                                G[:, mx, :, 0:C], G[:, sa, :, 0:C], G[:, sb_, :, 0:C], ALU.max))
                dve.wait_ge(*last)
                note(dve.engine_nop(), sorted_ready)

            def finish(g):
                k, n, q0 = groups[g]
                dve.wait_ge(y_ready, g + 1)
                if 2 <= g < MG + 2:
                    dve.wait_ge(out_done[g % 2], 16 * min(g // 2, MG // 2))
                if g >= MG + 2:
                    dve.wait_ge(scattered[g - 2 - MG], 16 * groups[g - 2][1])
                y = y_ps[:, 0:n, :]
                if g < MG:
                    mk = mask[:, g * T:(g + 1) * T]
                    xs = x_all[:, g * T:(g + 1) * T, :]
                else:
                    mk = rec_of(g, R_MASK, R_MASK + 1).rearrange("p t a -> p (t a)")
                    xs = rec_of(g, R_X, R_X + C)
                step(nc.vector.tensor_tensor(fin2[:, 0:n, :], y, over(mk, [P, n, C]), ALU.mult))
                note(nc.vector.tensor_tensor(fin[:, g % 2, 0:n, :], fin2[:, 0:n, :], xs, ALU.add), fin_ready)

            step(nc.vector.memset(padrow[:, 0:C], BIG))
            note(nc.vector.memset(padrow[:, C:TW], 0.0), pads_made)
            step(nc.vector.memset(padrec[:, 0:LIST + 1], float(PAD)))
            note(nc.vector.memset(padrec[:, LIST + 1:RW], 0.0), pads_made)
            dve.wait_ge(small_in, 16 * 5)
            note(nc.vector.tensor_copy(maskr[:, :], mask8[:, :]), mask_float)

            tpos = crow[:, 2, :]
            statistics(0, 1)
            for b in range(AHEAD):
                if b == 1:
                    statistics(1, B)
                normalise(b)
                list_rows(b)
                dilate(b)
            dve.wait_ge(consts_made, T + 1)
            step(nc.vector.tensor_scalar(tpos, gid[:, :], gid[:, 0:1], 1.0 / P, ALU.subtract, ALU.mult))
            for g in range(len(groups)):
                sort_group(g)
                if g >= 1:
                    finish(g - 1)
                if g + AHEAD < MG:
                    normalise(g + AHEAD)
                    list_rows(g + AHEAD)
                    dilate(g + AHEAD)
                if g + AHEAD == MG - 1:
                    pick_crowded()
                if g == MG - 2:
                    crowded_indices()
            finish(len(groups) - 1)
            with dve.If(general_taken(dve) > 0):
                general_path()

        @block.scalar
        def _(act):
            act.wait_ge(pads_made, 2)
            for b in range(B):
                act.dma_start(tables[b][N:N + 1, :], padrow[:, :]).then_inc(pads_out, 16)
            act.dma_start(table[PAD:PAD + 1, :], padrow[:, :]).then_inc(pads_out, 16)
            act.dma_start(records[PAD:PAD + 1, :], padrec[:, :]).then_inc(pads_out, 16)

            def first(b):
                if b < 2:
                    part = var[:, 0:T] if b == 0 else var[:, T:NT]
                    act.wait_ge(var_ready, b + 1)
                    act.activation(part, part, ACT.Sqrt).then_inc(std_ready, 1)
                act.wait_ge(records_ready, b + 1)
                act.dma_start(tables[b][0:N, :].rearrange("(t p) w -> p t w", p=P),
                              rec[:, b % NREC, :, R_H:REC]).then_inc(stored[b % NREC], 16)
                act.dma_start(table_t[:, b * T:(b + 1) * T, :],
                              rec[:, b % NREC, :, R_H:REC]).then_inc(stored[b % NREC], 16)
                act.dma_start(records_t[:, b * T:(b + 1) * T, :],
                              rec[:, b % NREC, :, 0:RW]).then_inc(stored[b % NREC], 16)

            def own_value(g):
                k, n, q0 = groups[g]
                if g >= MG:
                    act.wait_ge(crowd_idx, 1)
                if 2 <= g < MG:
                    act.wait_ge(weighted, g - 1)
                act.activation(slots_of(g)[:, k - 1, :, 0:C], rec_of(g, R_H, R_H + C),
                               ACT.Copy).then_inc(self_in, 1)

            def weigh(g):
                k, n, q0 = groups[g]
                top = top_rank(k) + 1
                _, where = network_steps(k, MSP if g < MG else OSP)
                act.wait_ge(sorted_ready, g + 1)
                if g >= 1:
                    act.wait_ge(summed, g)
                for r in range(top):
                    for i in range(n):
                        last = act.activation(wsort[:, r * n + i, :], slots_of(g)[:, where[r], i, 0:C], ACT.Copy,
                                              scale=wgt[:, g % 2, i, r:r + 1])
                last.then_inc(weighted, 1)

            def mlp(g):
                k, n, q0 = groups[g]
                cols = n * P
                act.wait_ge(summed, g + 1)
                act.activation(oT[:, 0:cols], oT_ps[:, 0:cols], ACT.Copy).then_inc(sum_out, 1)
                act.wait_ge(hidden, g + 1)
                act.activation(h1[:, 0:cols], h1_ps[:, 0:cols], ACT.Relu, bias=b1s[:, 0:1]).then_inc(hidden_out, 1)

            def store(g):
                if g < MG:
                    act.wait_ge(fin_ready, g + 1)
                    act.dma_start(out_t[:, g * T:(g + 1) * T, :], fin[:, g % 2, :, :]).then_inc(out_done[g % 2], 16)

            act.wait_ge(small_in, 16 * 5)
            for b in range(AHEAD):
                first(b)
            own_value(0)
            own_value(1)
            for g in range(len(groups)):
                weigh(g)
                if g + 2 < len(groups):
                    own_value(g + 2)
                mlp(g)
                if g + AHEAD < MG:
                    first(g + AHEAD)
                if g >= 1:
                    store(g - 1)
            for i in range(2):
                act.wait_ge(out_done[i], 16 * (MG // 2))
            with act.If(general_taken(act) > 0):
                act.wait_ge(all_stored, 1)
                with act.Fori(0, B) as b:
                    act.wait_ge(g_hT_ready, b + 1)
                    act.activation(oT[:, :], h1_ps[0:C, :], ACT.Copy).then_inc(g_hT_out, 1)
                    act.wait_ge(g_hT_stored, 16 * (b + 1))
                    act.wait_ge(g_sum_ready, b + 1)
                    act.activation(oT[:, :], oT_ps, ACT.Copy).then_inc(g_sum_out, 1)
                    act.wait_ge(g_hid_ready, b + 1)
                    act.activation(h1[:, :], h1_ps[:, :], ACT.Relu, bias=b1s[:, 0:1]).then_inc(g_hid_out, 1)

        @block.tensor
        def _(pe):
            pe.wait_ge(consts_made, T + 1)
            pe.wait_ge(mask_float, 1)
            nc.tensor.transpose(m_ps[:, 0:NT], maskr[:, :], ident[0:NT, 0:NT]).then_inc(mask_turned, 1)
            pe.wait_ge(small_in, 16 * 5)
            for g, (k, n, q0) in enumerate(groups):
                top = top_rank(k) + 1
                pe.wait_ge(weighted, g + 1)
                if g >= 1:
                    pe.wait_ge(sum_out, g)
                for i in range(n):
                    o = oT_ps[:, i * P:(i + 1) * P]
                    nc.tensor.matmul(o, rec_of(g, R_H, R_H + C)[:, i, :], ident[:, :], start=True, stop=False)
                    for r in range(top):
                        last = nc.tensor.matmul(o, wsort[:, r * n + i, :], ident[:, :], start=False, stop=r == top - 1)
                last.then_inc(summed, 1)
                pe.wait_ge(sum_out, g + 1)
                if g >= 1:
                    pe.wait_ge(hidden_out, g)
                for a in range(0, n * P, 512):
                    z = min(a + 512, n * P)
                    last = nc.tensor.matmul(h1_ps[:, a:z], w1s[:, :], oT[:, a:z], start=True, stop=True)
                last.then_inc(hidden, 1)
                pe.wait_ge(hidden_out, g + 1)
                if g >= 1:
                    pe.wait_ge(fin_ready, g)
                for i in range(n):
                    nc.tensor.matmul(y_ps[:, i, :], ones1[:, :], b2s[:, :], start=True, stop=False)
                    last = nc.tensor.matmul(y_ps[:, i, :], h1[:, i * P:(i + 1) * P], w2s[:, :],
                                            start=False, stop=True)
                last.then_inc(y_ready, 1)
                if g == PICK:
                    pe.wait_ge(flag_part, 1)
                    nc.tensor.matmul(m_ps[0:1, 0:1], crowd_flag[:, 0:1], crowd_flag[:, 1:2],
                                     start=True, stop=True).then_inc(flag_sum, 1)
            with pe.If(general_taken(pe) > 0):
                pe.wait_ge(all_stored, 1)
                pe.wait_ge(g_const, 2)
                with pe.Fori(0, B) as b:
                    pe.wait_ge(g_h_in, 16 * (b + 1))
                    pe.sem_inc(g_passed, 1)
                    for i in range(T):
                        last = nc.tensor.transpose(h1_ps[0:C, i * P:(i + 1) * P], g_h[:, i, :], ident[:, :])
                    last.then_inc(g_hT_ready, 1)
                    pe.wait_ge(g_gone_ready, b + 1)
                    for i in range(T):
                        pe.wait_ge(g_flip_used, b * T + i + 1)
                        for k in range(T):
                            last = nc.tensor.transpose(flip_ps[:, k * P:(k + 1) * P],
                                                       g_gone[:, k, i * P:(i + 1) * P], g_ident)
                        last.then_inc(g_flip_ready, 1)
                    pe.wait_ge(g_valid_ready, b + 1)
                    for i in range(T):
                        pe.wait_ge(g_turn_out, b * T + i + 1)
                        for k in range(T):
                            last = nc.tensor.transpose(flip_ps[:, k * P:(k + 1) * P],
                                                       g_valid[:, k, i * P:(i + 1) * P], g_ident)
                        last.then_inc(g_turn_ready, 1)
                    pe.wait_ge(g_hT_out, b + 1)
                    pe.sem_inc(g_passed, 1)
                    with pe.Fori(0, C) as c:
                        pe.wait_ge(g_less_ready, b * C + c + 1)
                        for i in range(T):
                            if i >= 2:
                                pe.wait_ge(g_count_used, (b * C + c) * T + i - 1)
                            for half in range(2):
                                for k in range(T):
                                    last = nc.tensor.matmul(
                                        (oT_full, h1_ps)[i % 2][:, half * 512:(half + 1) * 512],
                                        g_turned[:, k, i * P:(i + 1) * P], g_less[:, k, half * 512:(half + 1) * 512],
                                        start=k == 0, stop=k == T - 1)
                            last.then_inc(g_count_ready, 1)
                    pe.wait_ge(g_agg_ready, b + 1)
                    for i in range(T):
                        o = oT_ps[:, i * P:(i + 1) * P]
                        nc.tensor.matmul(o, g_h[:, i, :], ident[:, :], start=True, stop=False)
                        last = nc.tensor.matmul(o, g_agg[:, i, :], ident[:, :], start=False, stop=True)
                    last.then_inc(g_sum_ready, 1)
                    pe.wait_ge(g_sum_out, b + 1)
                    for a in range(0, N, 512):
                        last = nc.tensor.matmul(h1_ps[:, a:a + 512], w1s[:, :], oT[:, a:a + 512],
                                                start=True, stop=True)
                    last.then_inc(g_hid_ready, 1)
                    pe.wait_ge(g_hid_out, b + 1)
                    for i in range(T):
                        nc.tensor.matmul(y_ps[:, i, :], ones1[:, :], b2s[:, :], start=True, stop=False)
                        last = nc.tensor.matmul(y_ps[:, i, :], h1[:, i * P:(i + 1) * P], w2s[:, :],
                                                start=False, stop=True)
                    last.then_inc(g_y_ready, 1)


_INS = ['x', 'adj', 'nodemask', 'L0_gnn_W1', 'L0_gnn_b1', 'L0_gnn_W2', 'L0_gnn_b2']


def kernel(**inputs):
    import numpy as _np
    import concourse.bacc as _bacc
    from concourse import mybir as _mybir
    from concourse.bass_utils import run_bass_kernel_spmd as _run

    nc = _bacc.Bacc("TRN2", target_bir_lowering=False, num_devices=1)
    arrays, args = {}, []
    for name in _INS:
        a = _np.ascontiguousarray(inputs[name])
        if a.dtype == _np.bool_:
            a = a.view(_np.uint8)
        arrays[f"in_{name}"] = a
        args.append(nc.dram_tensor(f"in_{name}", a.shape, _mybir.dt.from_np(a.dtype), kind="ExternalInput").ap())
    shape = inputs['x'].shape
    out = nc.dram_tensor("out_0", shape, _mybir.dt.float32, kind="ExternalOutput").ap()
    quantile_gnn(nc, *args, out)
    r = _run(nc, [arrays], core_ids=[0])
    return r.results[0]["out_0"]
```

```python
import concourse.bass as bass
from concourse import mybir
from contextlib import ExitStack

FP32 = mybir.dt.float32
FP16 = mybir.dt.float16
BF16 = mybir.dt.bfloat16
I32 = mybir.dt.int32
ALU = mybir.AluOpType
ACT = mybir.ActivationFunctionType
AX = mybir.AxisListType

NETWORKS = {
    8: [(0, 2), (1, 3), (4, 6), (5, 7), (0, 4), (1, 5), (2, 6), (3, 7), (0, 1), (2, 3), (4, 5), (6, 7),
        (2, 4), (3, 5), (1, 4), (3, 6), (1, 2), (3, 4), (5, 6)],
    10: [(0, 8), (1, 9), (2, 7), (3, 5), (4, 6), (0, 2), (1, 4), (5, 8), (7, 9), (0, 3), (2, 4), (5, 7),
         (6, 9), (0, 1), (3, 6), (8, 9), (1, 5), (2, 3), (4, 8), (6, 7), (1, 2), (3, 5), (4, 6), (7, 8),
         (2, 3), (4, 5), (6, 7), (3, 4), (5, 6)],
    12: [(0, 8), (1, 7), (2, 6), (3, 11), (4, 10), (5, 9), (0, 1), (2, 5), (3, 4), (6, 9), (7, 8), (10, 11),
         (0, 2), (1, 6), (5, 10), (9, 11), (0, 3), (1, 2), (4, 6), (5, 7), (8, 11), (9, 10), (1, 4), (3, 5),
         (6, 8), (7, 10), (1, 3), (2, 5), (6, 9), (8, 10), (2, 3), (4, 5), (6, 7), (8, 9), (4, 6), (5, 7),
         (3, 4), (5, 6), (7, 8)],
}


def odd_even_merge(n):
    net, p = [], 1
    while p < n:
        k = p
        while k >= 1:
            for j in range(k % p, n - k, 2 * k):
                for i in range(min(k, n - j - k)):
                    if (i + j) // (2 * p) == (i + j + k) // (2 * p):
                        net.append((i + j, i + j + k))
            k //= 2
        p *= 2
    return net


NETWORKS[17] = odd_even_merge(17)


def top_rank(slots):
    return -(-3 * (slots - 1) // 4)


def network_steps(slots, spares):
    wanted = set(range(top_rank(slots) + 1))
    kept = []
    for a, b in reversed(NETWORKS[slots]):
        if a in wanted or b in wanted:
            kept.append((a, b, a in wanted, b in wanted))
            wanted |= {a, b}
    kept.reverse()
    at = list(range(slots))
    free = list(range(slots, slots + spares))
    layers = []
    while kept:
        layer, busy, freed, later = [], set(), [], []
        for a, b, low, high in kept:
            if a in busy or b in busy or not free:
                later.append((a, b, low, high))
                busy |= {a, b}
                continue
            busy |= {a, b}
            mn = free.pop(0) if low else None
            layer.append((at[a], at[b], mn, at[b] if high else None))
            if low:
                freed.append(at[a])
                at[a] = mn
        free += freed
        kept = later
        layers.append(layer)
    return layers, at


def quantile_gnn(nc, x, adj, nodemask, W1, b1, W2, b2, out):
    B, N, C = x.shape
    H = W1.shape[1]
    P = 128
    T = N // P
    NT = B * T
    BIG = 1e30
    PAD = B * N
    LIST = 16
    KM = 8
    R_ID, R_CNT, R_KEY, R_MASK = LIST, LIST + 1, LIST + 2, LIST + 3
    R_X = LIST + 4
    R_H = R_X + C
    R_REM = R_H + C
    RW = R_REM
    TW = C + 4
    REC = RW + 4
    TAUS = [(0.25, 0.25), (0.5, 0.5), (0.75, 0.25)]
    CLASSES = [(0, 17, 2), (2, 12, 3), (5, 10, 3), (8, 10, 3)]
    NOV = 11
    CH = 2
    NRING = 6
    NCH = NT // CH
    NSIGN = 3
    FOLD = 4
    NF = N // FOLD
    NBANK = 4
    AHEAD = 3
    NREC = AHEAD + 1

    MSP, OSP = 4, 3
    groups = [(KM, T, None)] * B + [(k, n, q0) for q0, k, n in CLASSES]
    MG = B
    PICK = MG - 1 - AHEAD

    x_t = x.rearrange("b (t p) c -> p (b t) c", p=P)
    out_t = out.rearrange("b (t p) c -> p (b t) c", p=P)
    out_rows = out.rearrange("b n c -> (b n) c")
    adj_t = adj.rearrange("b (t p) j -> p (b t) j", p=P)
    tables = [nc.dram_tensor(f"table{b}", [N + 1, TW], FP32, kind="Internal").ap() for b in range(B)]
    table = nc.dram_tensor("table", [PAD + 1, TW], FP32, kind="Internal").ap()
    records = nc.dram_tensor("records", [PAD + 1, RW], FP32, kind="Internal").ap()
    table_t = table[0:PAD, :].rearrange("(t p) w -> p t w", p=P)
    h_turned = nc.dram_tensor("h_turned", [B, C, N], FP32, kind="Internal").ap()
    records_t = records[0:PAD, :].rearrange("(t p) w -> p t w", p=P)

    ctx = ExitStack()
    with ctx:
        def sb(name, shape, dt):
            return ctx.enter_context(nc.sbuf_tensor(name, shape, dt))

        def pb(name, shape):
            return ctx.enter_context(nc.psum_tensor(name, shape, FP32))

        def sem(name):
            return ctx.enter_context(nc.semaphore(name))

        x_all = sb("x_all", [P, NT, C], FP32)
        signs = sb("signs", [P, NSIGN, N], FP16)
        adj_ring = sb("adj_ring", [P, NRING, CH, N], FP32)
        folded2 = sb("folded2", [P, 2, NF], FP32)
        entries = sb("entries", [P, T, LIST], FP32)
        entry_int = sb("entry_int", [P, T, LIST], I32)
        entry_bits = sb("entry_bits", [P, T, LIST], I32)
        entry_key = sb("entry_key", [P, T, LIST], I32)
        one_bit = sb("one_bit", [P, FOLD, T, LIST], I32)
        cand = sb("cand", [P, T, FOLD, LIST], FP32)
        cand2 = sb("cand2", [P, 2, FOLD * LIST], FP32)
        lists = sb("lists", [P, T, LIST], FP32)
        tmpa = sb("tmpa", [P, T, LIST], FP32)
        tmpb = sb("tmpb", [P, T, LIST], FP32)
        tmpc = sb("tmpc", [P, T, LIST], FP32)
        st = sb("st", [P, 5, T], FP32)
        less_mean = sb("less_mean", [P, NT], FP32)
        var = sb("var", [P, NT], FP32)
        xc = sb("xc", [P, T, C], FP32)
        rec = sb("rec", [P, NREC, T, REC], FP32)
        nidx = sb("nidx", [P, NREC, T, KM - 1], I32)
        unlisted = sb("unlisted", [P, NT], FP32)
        degree = sb("degree", [P, NT], FP32)
        gat = sb("gat", [P, 2, KM + MSP, T, TW], FP32)
        wsort = sb("wsort", [P, max(n * (top_rank(k) + 1) for k, n, _ in groups), C], FP32)
        wmax = max(n * (top_rank(k) + 1) for k, n, _ in groups)
        wgt = sb("wgt", [P, 2, wmax], FP32)
        fl = sb("fl", [P, 3, max((k - 1) * n for k, n, _ in groups)], FP32)
        s2 = sb("s2", [P, 4, T], FP32)
        tent = sb("tent", [P, 2, 3 * wmax], FP32)
        pos = sb("pos", [P, 3, T], FP32)
        tau3 = sb("tau3", [P, 3], FP32)
        share3 = sb("share3", [P, 3], FP32)
        key_row = sb("key_row", [1, NF], FP16)
        ones_h = sb("ones_h", [1, P], FP16)
        eyes = sb("eyes", [P, FOLD, P], FP16)
        off_diag = sb("off_diag", [P, P], FP32)
        oT = sb("oT", [C, T * P], FP32)
        h1 = sb("h1", [H, T * P], FP32)
        fin = sb("fin", [P, 2, T, C], FP32)
        fin2 = sb("fin2", [P, T, C], FP32)
        ident = sb("ident", [P, P], FP32)
        w1s = sb("w1s", [C, H], FP32)
        b1s = sb("b1s", [H, 1], FP32)
        w2s = sb("w2s", [H, C], FP32)
        b2s = sb("b2s", [1, C], FP32)
        ones1 = sb("ones1", [1, P], FP32)
        mask8 = sb("mask8", [NT, P], mybir.dt.uint8)
        maskr = sb("maskr", [NT, P], FP32)
        mask = sb("mask", [P, NT], FP32)
        kk = sb("kk", [P, LIST], FP32)
        kpos = sb("kpos", [P, LIST], FP32)
        gid = sb("gid", [P, NT], FP32)
        ownkey = sb("ownkey", [P, T], FP32)
        padrow = sb("padrow", [1, TW], FP32)
        padrec = sb("padrec", [1, RW], FP32)
        crow = sb("crow", [P, 3, NT], FP32)
        crowk = sb("crowk", [P, 16], FP32)
        crowi = sb("crowi", [P, 16], I32)
        crowf = sb("crowf", [P, 16], FP32)
        rid = sb("rid", [P, NOV], I32)
        rv = sb("rv", [P, NOV, RW], FP32)
        rvi = sb("rvi", [P, NOV, LIST + 1], I32)

        adj_flat = adj_ring[:, :, :, :].rearrange("p a b n -> p (a b n)")
        ov_gat, at = [], 0
        for q0, k, n in CLASSES:
            size = (k + OSP) * n * TW
            ov_gat.append(adj_flat[:, at:at + size].rearrange("p (s t w) -> p s t w", s=k + OSP, t=n))
            at += size
        assert at <= NRING * CH * N

        def ring_part(k, dt, words):
            part = adj_flat[:, k:k + words]
            return part if dt == FP32 else part.bitcast(dt)

        g_adj = ring_part(0, FP32, N)
        g_scan = ring_part(N, FP32, N)
        g_tmp = ring_part(2 * N, FP32, N)
        g_row = ring_part(3 * N, FP32, N)
        g_valid = ring_part(4 * N, BF16, T * N // 2).rearrange("p (t n) -> p t n", t=T)
        g_ones = ring_part(8 * N, BF16, N // 2)
        g_flip = ring_part(9 * N, BF16, N // 2)
        g_ident = ring_part(10 * N, BF16, P // 2)
        g_off = ring_part(10 * N + P, BF16, P // 2)
        g_small = ring_part(11 * N, FP32, 512)
        gat_flat = gat[:, :, :, :, :].rearrange("p a s t w -> p (a s t w)")
        g_gone = gat_flat[:, 0:T * N // 2].bitcast(BF16).rearrange("p (t n) -> p t n", t=T)
        g_less = g_gone
        g_turned = gat_flat[:, T * N // 2:T * N].bitcast(BF16).rearrange("p (t n) -> p t n", t=T)
        g_h = gat_flat[:, T * N:T * N + T * C].rearrange("p (t c) -> p t c", t=T)
        g_agg = gat_flat[:, T * N + T * C:T * N + 2 * T * C].rearrange("p (t c) -> p t c", t=T)

        key_ps = pb("key_ps", [P, NBANK, 512])
        acc_ps = pb("acc_ps", [P, T * P])
        oT_ps = acc_ps[0:C, :]
        h1_ps = acc_ps
        flip_ps = key_ps[:, 0, :].bitcast(BF16)
        count_ps = [key_ps[:, 2 * i:2 * i + 2, :].rearrange("p a n -> p (a n)") for i in range(2)]
        y_ps = pb("y_ps", [P, T, C])
        m_ps = pb("m_ps", [P, 512])
        crowd_flag = sb("crowd_flag", [P, 4], FP32)
        general = sb("general", [1, 1], I32)

        def columns(g):
            return sum(n for _, n, _ in groups[:g])

        def slots_of(g):
            return gat[:, g % 2, :, :, :] if g < MG else ov_gat[g - MG]

        def rec_of(g, a, z):
            if g < MG:
                return rec[:, g % NREC, :, a:z]
            k, n, q0 = groups[g]
            return rv[:, q0:q0 + n, a:z]

        x_in = sem("x_in")
        small_in = sem("small_in")
        adj_in = [sem(f"adj_in{i}") for i in range(NRING)]
        signed = sem("signed")
        keyed_ready = sem("keyed_ready")
        tile_taken = sem("tile_taken")
        diag_clear = sem("diag_clear")
        relued = sem("relued")
        relued_early = sem("relued_early")
        x_copied = sem("x_copied")
        consts_made = sem("consts_made")
        pool_step = sem("pool_step")
        dve_step = sem("dve_step")
        pads_made = sem("pads_made")
        pads_out = sem("pads_out")
        mask_float = sem("mask_float")
        mask_turned = sem("mask_turned")
        var_ready = sem("var_ready")
        std_ready = sem("std_ready")
        records_ready = sem("records_ready")
        stored = [sem(f"stored{i}") for i in range(NREC)]
        table_stored = [sem(f"table_stored{i}") for i in range(NREC)]
        self_in = sem("self_in")
        gathered = [sem(f"gathered{i}") for i in range(2)] + [sem(f"gathered_ov{i}") for i in range(len(CLASSES))]
        crowd_ready = sem("crowd_ready")
        recs_gathered = sem("recs_gathered")
        crowd_idx = sem("crowd_idx")
        sorted_ready = sem("sorted_ready")
        weighted = sem("weighted")
        summed = sem("summed")
        sum_out = sem("sum_out")
        hidden = sem("hidden")
        hidden_out = sem("hidden_out")
        y_ready = sem("y_ready")
        fin_ready = sem("fin_ready")
        out_done = [sem(f"out_done{i}") for i in range(2)]
        scattered = [sem(f"scattered{i}") for i in range(len(CLASSES))]

        flag_part = sem("flag_part")
        flag_sum = sem("flag_sum")
        flag_ready = sem("flag_ready")
        all_stored = sem("all_stored")
        g_const = sem("g_const")
        g_adj_in = sem("g_adj_in")
        g_adj_used = sem("g_adj_used")
        g_gone_ready = sem("g_gone_ready")
        g_flip_ready = sem("g_flip_ready")
        g_flip_used = sem("g_flip_used")
        g_valid_ready = sem("g_valid_ready")
        g_turn_ready = sem("g_turn_ready")
        g_turn_out = sem("g_turn_out")
        g_h_in = sem("g_h_in")
        g_hT_ready = sem("g_hT_ready")
        g_hT_out = sem("g_hT_out")
        g_hT_stored = sem("g_hT_stored")
        g_row_in = sem("g_row_in")
        g_less_ready = sem("g_less_ready")
        g_count_ready = sem("g_count_ready")
        g_count_used = sem("g_count_used")
        g_chan_done = sem("g_chan_done")
        g_agg_ready = sem("g_agg_ready")
        g_sum_ready = sem("g_sum_ready")
        g_sum_out = sem("g_sum_out")
        g_hid_ready = sem("g_hid_ready")
        g_hid_out = sem("g_hid_out")
        g_y_ready = sem("g_y_ready")
        g_fin_ready = sem("g_fin_ready")
        g_out_done = sem("g_out_done")
        g_passed = sem("g_passed")

        block = ctx.enter_context(nc.Block())

        def general_taken(eng):
            eng.wait_ge(flag_ready, 1)
            return eng.value_load(general[0:1, 0:1], min_val=0, max_val=1)

        @block.sync
        def _(sp):
            sp.dma_start(x_all[:, 0:T, :], x_t[:, 0:T, :]).then_inc(x_in, 16)
            for c in range(2):
                sp.dma_start(adj_ring[:, c, :, :], adj_t[:, c * CH:(c + 1) * CH, :]).then_inc(adj_in[c], 16)
            sp.dma_start(mask8[:, :], nodemask.rearrange("b (t p) -> (b t) p", p=P)).then_inc(small_in, 16)
            sp.dma_start(w1s[:, :], W1).then_inc(small_in, 16)
            sp.dma_start(b1s[:, :], b1.rearrange("(h a) -> h a", a=1)).then_inc(small_in, 16)
            sp.dma_start(w2s[:, :], W2).then_inc(small_in, 16)
            sp.dma_start(b2s[:, :], b2.rearrange("(a c) -> a c", a=1)).then_inc(small_in, 16)
            for c in range(2, NCH):
                if c == T // CH:
                    sp.wait_ge(x_in, 16)
                    sp.dma_start(x_all[:, T:NT, :], x_t[:, T:NT, :]).then_inc(x_in, 16)
                if c >= NRING:
                    sp.wait_ge(signed, (c - NRING + 1) * CH)
                sp.dma_start(adj_ring[:, c % NRING, :, :],
                             adj_t[:, c * CH:(c + 1) * CH, :]).then_inc(adj_in[c % NRING], 16)

            with sp.If(general_taken(sp) > 0):
                sp.wait_ge(all_stored, 1)
                with sp.Fori(0, B) as b:
                    sp.dma_start(g_h, records_t[:, bass.ds(b * T, T), R_H:R_H + C]).then_inc(g_h_in, 16)
                    for i in range(T):
                        sp.wait_ge(g_adj_used, b * T + i + 1)
                        sp.dma_start(g_adj, adj_t[:, bass.ds(b * T + i, 1), :].rearrange(
                            "p t n -> p (t n)")).then_inc(g_adj_in, 16)
                    sp.wait_ge(g_hT_out, b + 1)
                    sp.dma_start(h_turned[bass.ds(b, 1), :, :].rearrange("b c n -> c (b n)"),
                                 oT[:, :]).then_inc(g_hT_stored, 16)
                    sp.wait_ge(g_hT_stored, 16 * (b + 1))
                    sp.sem_inc(g_passed, 1)
                    with sp.Fori(0, C) as c:
                        sp.wait_ge(g_chan_done, b * C + c + 1)
                        sp.dma_start(g_row, h_turned[bass.ds(b, 1), bass.ds(c, 1), :].rearrange(
                            "b c n -> (b c) n").partition_broadcast(P)).then_inc(g_row_in, 16)
                    sp.wait_ge(g_fin_ready, b + 1)
                    sp.dma_start(out_t[:, bass.ds(b * T, T), :], fin[:, 0, :, :]).then_inc(g_out_done, 16)
                    sp.wait_ge(g_out_done, 16 * (b + 1))
                    sp.sem_inc(g_passed, 1)

        @block.gpsimd
        def _(pool):
            pool.memset(off_diag[:, :], 1.0).then_inc(pool_step, 1)
            pool.memset(ident[:, :], 0.0).then_inc(pool_step, 1)
            pool.memset(eyes[:, :, :], 0.0).then_inc(pool_step, 1)
            pool.memset(ones_h[:, :], 1.0)
            pool.iota(key_row[:, :], [[-1, NF]], base=NF, channel_multiplier=0,
                      allow_small_or_imprecise_dtypes=True)
            pool.wait_ge(pool_step, 3)
            for m, value in ((off_diag[:, :], 0.0), *((eyes[:, q, :], float(N << q)) for q in range(FOLD)),
                             (ident[:, :], 1.0)):
                pool.affine_select(out=m, in_=m, compare_op=ALU.not_equal, fill=value,
                                   base=0, pattern=[[-1, P]], channel_multiplier=1).then_inc(consts_made, 1)
            pool.iota(kk[:, :], [[1, LIST]], base=1, channel_multiplier=0,
                      allow_small_or_imprecise_dtypes=True)
            pool.iota(kpos[:, :], [[1, LIST]], base=0, channel_multiplier=0,
                      allow_small_or_imprecise_dtypes=True)
            pool.iota(gid[:, :], [[P, NT]], base=0, channel_multiplier=1,
                      allow_small_or_imprecise_dtypes=True)
            pool.iota(ownkey[:, :], [[-P, T]], base=N, channel_multiplier=-1,
                      allow_small_or_imprecise_dtypes=True)
            for q, (tau, share) in enumerate(TAUS):
                pool.memset(tau3[:, q:q + 1], tau)
                pool.memset(share3[:, q:q + 1], share)
            pool.memset(ones1[:, :], 1.0).then_inc(consts_made, 1)

            def gather(g):
                k, n, q0 = groups[g]
                for i in range(n):
                    for s in range(k - 1):
                        idx = nidx[:, g % NREC, i, s:s + 1] if g < MG else rvi[:, q0 + i, s:s + 1]
                        pool.indirect_dma_start(
                            out=slots_of(g)[:, s, i, :], out_offset=None,
                            in_=tables[g][:, :] if g < MG else table[:, :],
                            in_offset=bass.IndirectOffsetOnAxis(ap=idx, axis=0),
                            bounds_check=N if g < MG else PAD, oob_is_err=False,
                        ).then_inc(gathered[g % 2 if g < MG else 2 + g - MG], 16)

            pool.wait_ge(pads_out, 16 * (B + 2))
            for g in range(MG):
                if g >= 2:
                    pool.wait_ge(weighted, columns(g - 1))
                pool.wait_ge(table_stored[g % NREC], 16 * (g // NREC + 1))
                if g == MG - 1:
                    pool.wait_ge(crowd_ready, 1)
                    for i in range(NREC):
                        pool.wait_ge(stored[i], 32 * (MG // NREC))
                    for q in range(NOV):
                        pool.indirect_dma_start(
                            out=rv[:, q, :], out_offset=None, in_=records[:, :],
                            in_offset=bass.IndirectOffsetOnAxis(ap=rid[:, q:q + 1], axis=0),
                            bounds_check=PAD, oob_is_err=False).then_inc(recs_gathered, 16)
                gather(g)
            pool.wait_ge(crowd_idx, 1)
            for g in range(MG, len(groups)):
                gather(g)
            for i in range(2):
                pool.wait_ge(out_done[i], 16 * (MG // 2))
            for g in range(MG, len(groups)):
                k, n, q0 = groups[g]
                pool.wait_ge(fin_ready, g + 1)
                for i in range(n):
                    pool.indirect_dma_start(
                        out=out_rows, out_offset=bass.IndirectOffsetOnAxis(
                            ap=rvi[:, q0 + i, LIST:LIST + 1], axis=0),
                        in_=fin[:, g % 2, i, :], in_offset=None,
                        bounds_check=PAD - 1, oob_is_err=False).then_inc(scattered[g - MG], 16)
            for g in range(MG, len(groups)):
                pool.wait_ge(scattered[g - MG], 16 * groups[g][1])
            pool.engine_nop().then_inc(all_stored, 1)

        @block.vector
        def _(dve):
            count = {}

            def note(ins, s=None):
                s = dve_step if s is None else s
                count[id(s)] = count.get(id(s), 0) + 1
                ins.then_inc(s, 1)
                return s, count[id(s)]

            def step(ins, s=None):
                dve.wait_ge(*note(ins, s))

            def row(i):
                return st[:, i, :]

            def over(ap, shape):
                return ap.unsqueeze(2).to_broadcast(shape)

            def statistics(b0, b1):
                dve.wait_ge(x_in, 16 if b0 == 0 else 32)
                for b in range(b0, b1):
                    cut = slice(b * T, (b + 1) * T)
                    xb = x_all[:, cut, :]
                    step(nc.vector.tensor_reduce(less_mean[:, cut], xb, axis=AX.X, op=ALU.add))
                    step(nc.vector.tensor_scalar(less_mean[:, cut], less_mean[:, cut], -1.0 / C, None, ALU.mult))
                    step(nc.vector.tensor_tensor(xc[:, :, :], xb, over(less_mean[:, cut], [P, T, C]), ALU.add))
                    step(nc.vector.tensor_tensor(xc[:, :, :], xc[:, :, :], xc[:, :, :], ALU.mult))
                    step(nc.vector.tensor_reduce(var[:, cut], xc[:, :, :], axis=AX.X, op=ALU.add))
                cut = slice(b0 * T, b1 * T)
                note(nc.vector.tensor_scalar(var[:, cut], var[:, cut], 1.0 / C, 1e-5, ALU.mult, ALU.add), var_ready)

            def normalise(b):
                cut = slice(b * T, (b + 1) * T)
                xb = x_all[:, cut, :]
                if b < 2:
                    dve.wait_ge(std_ready, b + 1)
                    part = var[:, 0:T] if b == 0 else var[:, T:NT]
                    step(nc.vector.reciprocal(part, part))
                if b >= NREC:
                    dve.wait_ge(stored[b % NREC], 32 * (b // NREC))
                    dve.wait_ge(table_stored[b % NREC], 16 * (b // NREC))
                    dve.wait_ge(summed, b - NREC + 1)
                else:
                    note(nc.vector.memset(rec[:, b, :, R_REM + 2:R_REM + 4], 0.0))
                r = rec[:, b % NREC, :, :]
                step(nc.vector.tensor_tensor(xc[:, :, :], xb, over(less_mean[:, cut], [P, T, C]), ALU.add))
                step(nc.vector.tensor_tensor(xc[:, :, :], xc[:, :, :], over(var[:, cut], [P, T, C]), ALU.mult))
                note(nc.vector.tensor_scalar(r[:, :, R_H:R_H + C], xc[:, :, :], 0.0, None, ALU.max))

            def clear_diagonal(t):
                c, i = t // CH, t % T
                dve.wait_ge(adj_in[c % NRING], 16 * (c // NRING + 1))
                d = adj_ring[:, c % NRING, t % CH, i * P:(i + 1) * P]
                note(nc.vector.tensor_tensor(d, d, off_diag[:, :], ALU.mult), diag_clear)

            def list_rows(b):
                for i in range(T):
                    t = b * T + i
                    v = key_ps[:, t % NBANK, 0:NF]
                    dve.wait_ge(keyed_ready, t + 1)
                    step(nc.vector.max(entries[:, i, 0:8], v))
                    step(nc.vector.match_replace(folded2[:, t % 2, :], entries[:, i, 0:8], v, 0.0), tile_taken)
                    last = note(nc.vector.max(entries[:, i, 8:16], folded2[:, t % 2, :]))
                    if t + T < NT:
                        clear_diagonal(t + T)
                dve.wait_ge(*last)
                step(nc.vector.tensor_copy(entry_int[:, :, :], entries[:, :, :]))
                note(nc.vector.tensor_scalar(entry_key[:, :, :], entry_int[:, :, :], N - 1, None, ALU.bitwise_and))
                step(nc.vector.tensor_scalar(entry_bits[:, :, :], entry_int[:, :, :], N.bit_length() - 1, None,
                                             ALU.logical_shift_right))
                for q in range(FOLD):
                    last = note(nc.vector.tensor_scalar(one_bit[:, q, :, :], entry_bits[:, :, :], q, 1,
                                                        ALU.logical_shift_right, ALU.bitwise_and))
                dve.wait_ge(*last)
                for q in range(FOLD):
                    last = note(nc.vector.scalar_tensor_tensor(
                        cand[:, :, q, :], entry_key[:, :, :], float(N - (q + 1) * NF), one_bit[:, q, :, :],
                        ALU.add, ALU.mult))
                dve.wait_ge(*last)
                for i in range(T):
                    v = cand[:, i, :, :].rearrange("p q e -> p (q e)")
                    step(nc.vector.max(lists[:, i, 0:8], v))
                    step(nc.vector.match_replace(cand2[:, i % 2, :], lists[:, i, 0:8], v, 0.0))
                    last = note(nc.vector.max(lists[:, i, 8:16], cand2[:, i % 2, :]))
                dve.wait_ge(*last)

            def dilate(b):
                r = rec[:, b % NREC, :, :]
                deg = degree[:, b * T:(b + 1) * T]
                L, full = lists[:, :, :], [P, T, LIST]
                if b == 0:
                    dve.wait_ge(consts_made, FOLD + 3)
                    dve.wait_ge(mask_turned, 1)
                    step(nc.vector.tensor_copy(mask[:, :], m_ps[:, 0:NT]))
                step(nc.vector.tensor_scalar(tmpa[:, :, :], L, 0.0, None, ALU.is_gt))
                step(nc.vector.tensor_reduce(deg, tmpa[:, :, :], axis=AX.X, op=ALU.add))
                cut = slice(b * T, (b + 1) * T)
                dve.wait_ge(signed, (b + 1) * T)
                note(nc.vector.tensor_tensor(unlisted[:, cut], unlisted[:, cut], deg, ALU.subtract))
                step(nc.vector.tensor_scalar(row(3), deg, 11.0, 6.0, ALU.is_ge, ALU.mult))
                step(nc.vector.scalar_tensor_tensor(row(3), deg, 13.0, row(3), ALU.is_ge, ALU.add))
                step(nc.vector.scalar_tensor_tensor(row(3), deg, 15.0, row(3), ALU.is_ge, ALU.add))
                step(nc.vector.tensor_tensor(row(3), row(3), mask[:, b * T:(b + 1) * T], ALU.mult))
                step(nc.vector.tensor_scalar(row(4), row(3), 2.0, None, ALU.mult))
                places = kk[:, :].unsqueeze(1).to_broadcast(full)
                for n, place in enumerate((row(3), row(4))):
                    step(nc.vector.tensor_tensor(tmpa[:, :, :], places, over(place, full), ALU.is_equal))
                    step(nc.vector.tensor_tensor(tmpb[:, :, :], tmpa[:, :, :], L, ALU.mult))
                    note(nc.vector.tensor_reduce(r[:, :, R_REM + n:R_REM + n + 1], tmpb[:, :, :], axis=AX.X,
                                                 op=ALU.add))
                    step(nc.vector.tensor_tensor(L, L, tmpb[:, :, :], ALU.subtract))
                step(nc.vector.tensor_scalar(tmpa[:, :, :], L, 0.0, None, ALU.is_gt))
                note(nc.vector.tensor_reduce(r[:, :, R_CNT:R_CNT + 1], tmpa[:, :, :], axis=AX.X, op=ALU.add))
                if b >= NREC:
                    dve.wait_ge(gathered[b % 2], 16 * T * (KM - 1) * ((b - NREC) // 2 + 1))
                note(nc.vector.tensor_scalar(nidx[:, b % NREC, :, :], lists[:, :, 0:KM - 1], -1.0, float(N),
                                             ALU.mult, ALU.add))
                step(nc.vector.tensor_scalar(tmpb[:, :, :], tmpa[:, :, :], float(b * N + N - PAD), None,
                                             ALU.mult))
                step(nc.vector.scalar_tensor_tensor(tmpc[:, :, :], L, -1.0, tmpb[:, :, :], ALU.mult, ALU.add))
                step(nc.vector.tensor_scalar(r[:, :, 0:LIST], tmpc[:, :, :], float(PAD), None, ALU.add))
                note(nc.vector.tensor_copy(r[:, :, R_ID], gid[:, b * T:(b + 1) * T]))
                note(nc.vector.tensor_copy(r[:, :, R_KEY], ownkey[:, :]))
                note(nc.vector.tensor_copy(r[:, :, R_MASK], mask[:, b * T:(b + 1) * T]), records_ready)

            def pick_crowded():
                k1, k2 = crow[:, 0, :], crow[:, 1, :]
                step(nc.vector.tensor_scalar(k1, degree[:, :], 1.0, float(NT), ALU.add, ALU.mult))
                step(nc.vector.tensor_tensor(k1, k1, tpos, ALU.add))
                step(nc.vector.scalar_tensor_tensor(k1, degree[:, :], float(KM - 1), k1, ALU.is_gt, ALU.mult))
                step(nc.vector.max(crowk[:, 0:8], k1))
                step(nc.vector.match_replace(k2, crowk[:, 0:8], k1, 0.0))
                step(nc.vector.max(crowk[:, 8:16], k2))
                step(nc.vector.tensor_copy(crowi[:, :], crowk[:, :]))
                step(nc.vector.tensor_scalar(crowi[:, :], crowi[:, :], NT - 1, None, ALU.bitwise_and))
                step(nc.vector.tensor_copy(crowf[:, :], crowi[:, :]))
                step(nc.vector.tensor_scalar(crowf[:, :], crowf[:, :], float(P), gid[:, 0:1], ALU.mult, ALU.add))
                step(nc.vector.tensor_scalar(crowf[:, :], crowf[:, :], float(-PAD), None, ALU.add))
                step(nc.vector.scalar_tensor_tensor(crowf[:, :], crowk[:, :], 0.0, crowf[:, :],
                                                    ALU.is_gt, ALU.mult))
                note(nc.vector.tensor_scalar(rid[:, :], crowf[:, 0:NOV], float(PAD), None, ALU.add), crowd_ready)

                f = crowd_flag
                step(nc.vector.tensor_reduce(f[:, 0:1], unlisted[:, :], axis=AX.X, op=ALU.max))
                step(nc.vector.tensor_scalar(f[:, 0:1], f[:, 0:1], 0.0, None, ALU.is_gt))
                step(nc.vector.scalar_tensor_tensor(f[:, 0:1], crowk[:, NOV:NOV + 1], 0.0, f[:, 0:1],
                                                    ALU.is_gt, ALU.max))
                for q0, k, n in CLASSES:
                    step(nc.vector.scalar_tensor_tensor(f[:, 0:1], crowk[:, q0:q0 + 1], float((k + 1) * NT),
                                                        f[:, 0:1], ALU.is_ge, ALU.max))
                note(nc.vector.memset(f[:, 1:2], 1.0), flag_part)

            def general_path():
                dve.wait_ge(all_stored, 1)
                nc.vector.memset(g_ones, 1.0).then_inc(g_const, 1)
                dve.wait_ge(g_const, 1)
                nc.vector.tensor_copy(g_ident, ident[:, :]).then_inc(g_const, 1)
                nc.vector.tensor_scalar(g_off, ident[:, :], -1.0, 1.0, ALU.mult, ALU.add).then_inc(g_const, 1)
                dve.wait_ge(g_const, 3)
                g_k = g_small[:, 64:64 + 6 * T].rearrange("p (t s) -> p t s", t=T)
                g_w = g_small[:, 128:128 + 6 * T].rearrange("p (t s) -> p t s", t=T)
                g_ki = g_small[:, 192:192 + 3 * T].bitcast(I32).rearrange("p (q t) -> p q t", q=3)
                g_kj = g_small[:, 216:216 + 3 * T].bitcast(I32).rearrange("p (q t) -> p q t", q=3)
                g_kf = g_small[:, 240:240 + 3 * T].rearrange("p (q t) -> p q t", q=3)
                g_kg = g_small[:, 264:264 + 3 * T].rearrange("p (q t) -> p q t", q=3)
                g_skip = g_small[:, 288:289]
                g_skipi = g_small[:, 289:290].bitcast(I32)
                g_two = g_small[:, 290:291]
                g_do = g_small[:, 291:292]
                g_cnt = g_small[:, 296:296 + T]
                g_q = g_small[:, 304:310]
                g_q2 = g_small[:, 310:316]

                def sure(ins):
                    dve.drain()

                for free in (g_adj_used, g_chan_done, g_flip_used, g_turn_out):
                    dve.sem_inc(free, 1)
                with dve.Fori(0, B) as b:
                    for i in range(T):
                        dve.wait_ge(g_adj_in, 16 * (b * T + i + 1))
                        nb, gone = g_valid[:, i, :], g_gone[:, i, :]
                        sure(nc.vector.tensor_scalar(nb, g_adj, 0.0, None, ALU.is_gt))
                        dve.sem_inc(g_adj_used, 1)
                        d = g_valid[:, i, i * P:(i + 1) * P]
                        sure(nc.vector.tensor_tensor(d, d, g_off, ALU.mult))
                        sure(nc.vector.tensor_tensor_scan(g_scan, g_ones, nb, 0.0, ALU.mult, ALU.add))
                        m = g_scan[:, N - 1:N]
                        sure(nc.vector.tensor_scalar(g_skipi, m, 1.0, None, ALU.add))
                        sure(nc.vector.tensor_scalar(g_skipi, g_skipi, 1, None, ALU.logical_shift_right))
                        sure(nc.vector.tensor_copy(g_skip, g_skipi))
                        sure(nc.vector.tensor_scalar(g_do, m, 10.0, None, ALU.is_gt))
                        sure(nc.vector.tensor_tensor(g_do, g_do, mask[:, bass.ds(b * T + i, 1)], ALU.mult))
                        sure(nc.vector.tensor_tensor(g_skip, g_skip, g_do, ALU.mult))
                        sure(nc.vector.tensor_scalar(g_two, g_skip, 2.0, None, ALU.mult))
                        sure(nc.vector.tensor_scalar(g_tmp, g_scan, g_skip, None, ALU.is_equal))
                        sure(nc.vector.scalar_tensor_tensor(g_tmp, g_scan, g_two, g_tmp, ALU.is_equal, ALU.add))
                        sure(nc.vector.tensor_tensor(gone, g_tmp, nb, ALU.mult))
                        sure(nc.vector.tensor_tensor(nb, nb, gone, ALU.subtract))
                    dve.sem_inc(g_gone_ready, 1)
                    for i in range(T):
                        v = g_valid[:, i, :]
                        dve.wait_ge(g_flip_ready, b * T + i + 1)
                        sure(nc.vector.tensor_scalar(g_flip, flip_ps, -1.0, 1.0, ALU.mult, ALU.add))
                        dve.sem_inc(g_flip_used, 1)
                        sure(nc.vector.tensor_tensor(v, v, g_flip, ALU.mult))
                        d = g_valid[:, i, i * P:(i + 1) * P]
                        sure(nc.vector.tensor_tensor(d, d, g_ident, ALU.add))
                        sure(nc.vector.tensor_reduce(g_cnt[:, i:i + 1], v, axis=AX.X, op=ALU.add))
                    dve.sem_inc(g_valid_ready, 1)
                    for q in range(3):
                        sure(nc.vector.tensor_scalar(g_ki[:, q, :], g_cnt, -1.0, float(q + 1), ALU.add, ALU.mult))
                    sure(nc.vector.tensor_scalar(g_kj, g_ki, 2, None, ALU.logical_shift_right))
                    sure(nc.vector.tensor_scalar(g_ki, g_ki, 3, None, ALU.bitwise_and))
                    sure(nc.vector.tensor_copy(g_kf, g_kj))
                    sure(nc.vector.tensor_copy(g_kg, g_ki))
                    for q, (tau, share) in enumerate(TAUS):
                        sure(nc.vector.tensor_copy(g_k[:, :, 2 * q], g_kf[:, q, :]))
                        sure(nc.vector.tensor_scalar(g_k[:, :, 2 * q + 1], g_kf[:, q, :], 1.0, None, ALU.add))
                        sure(nc.vector.tensor_scalar(g_w[:, :, 2 * q + 1], g_kg[:, q, :], share / 4, None, ALU.mult))
                        sure(nc.vector.tensor_scalar(g_w[:, :, 2 * q], g_kg[:, q, :], -share / 4, share,
                                                     ALU.mult, ALU.add))
                    for i in range(T):
                        dve.wait_ge(g_turn_ready, b * T + i + 1)
                        sure(nc.vector.tensor_copy(g_turned[:, i, :], flip_ps))
                        dve.sem_inc(g_turn_out, 1)
                    dve.wait_ge(g_h_in, 16 * (b + 1))
                    dve.sem_inc(g_passed, 1)
                    with dve.Fori(0, C) as c:
                        dve.wait_ge(g_row_in, 16 * (b * C + c + 1))
                        for i in range(T):
                            nc.vector.tensor_scalar(g_less[:, i, :], g_row, g_h[:, i, bass.ds(c, 1)], None, ALU.is_gt)
                        dve.drain()
                        dve.sem_inc(g_less_ready, 1)
                        for i in range(T):
                            ps = count_ps[i % 2]
                            dve.wait_ge(g_count_ready, (b * C + c) * T + i + 1)
                            for q in range(6):
                                sure(nc.vector.scalar_tensor_tensor(g_tmp, ps, g_k[:, i, q:q + 1], g_row,
                                                                    ALU.is_le, ALU.mult))
                                sure(nc.vector.tensor_reduce(g_q[:, q:q + 1], g_tmp, axis=AX.X, op=ALU.max))
                            dve.sem_inc(g_count_used, 1)
                            sure(nc.vector.tensor_tensor(g_q2, g_q, g_w[:, i, :], ALU.mult))
                            sure(nc.vector.tensor_reduce(g_agg[:, i, bass.ds(c, 1)], g_q2, axis=AX.X, op=ALU.add))
                        dve.sem_inc(g_chan_done, 1)
                    dve.sem_inc(g_agg_ready, 1)
                    dve.wait_ge(g_y_ready, b + 1)
                    sure(nc.vector.tensor_tensor(fin2[:, :, :], y_ps[:, :, :], over(mask[:, bass.ds(b * T, T)], [P, T, C]),
                                                 ALU.mult))
                    sure(nc.vector.tensor_tensor(fin[:, 0, :, :], fin2[:, :, :], x_all[:, bass.ds(b * T, T), :], ALU.add))
                    dve.sem_inc(g_fin_ready, 1)

            def crowded_indices():
                dve.wait_ge(recs_gathered, 16 * NOV)
                note(nc.vector.tensor_copy(rvi[:, :, :], rv[:, :, 0:LIST + 1]), crowd_idx)
                dve.wait_ge(flag_sum, 1)
                note(nc.vector.tensor_scalar(general[:, :], m_ps[0:1, 0:1], 0.0, None, ALU.is_gt), flag_ready)

            def sort_group(g):
                k, n, q0 = groups[g]
                top = top_rank(k) + 1
                G = slots_of(g)
                if g < MG:
                    dve.wait_ge(gathered[g % 2], 16 * T * (KM - 1) * (g // 2 + 1))
                else:
                    dve.wait_ge(gathered[2 + g - MG], 16 * n * (k - 1))
                body = G[:, 0:k - 1, :, 0:C].rearrange("p s t c -> p (s t) c")
                f = [fl[:, i, 0:(k - 1) * n].rearrange("p (s t) -> p s t", s=k - 1) for i in range(3)]
                own = rec_of(g, R_KEY, R_KEY + 1).rearrange("p t a -> p a t").to_broadcast([P, k - 1, n])
                note(nc.vector.tensor_tensor(f[0], G[:, 0:k - 1, :, C], own, ALU.is_equal))
                step(nc.vector.tensor_tensor(f[1], G[:, 0:k - 1, :, C + 1], own, ALU.is_equal))
                step(nc.vector.tensor_tensor(f[2], f[0], f[1], ALU.add))
                note(nc.vector.tensor_scalar(f[0], f[2], BIG, None, ALU.mult))
                step(nc.vector.tensor_reduce(s2[:, 0, 0:n], f[2].rearrange("p s t -> p t s"), axis=AX.X,
                                             op=ALU.add))
                step(nc.vector.tensor_tensor(s2[:, 1, 0:n], rec_of(g, R_CNT, R_CNT + 1).rearrange(
                    "p t a -> p (t a)"), s2[:, 0, 0:n], ALU.subtract))
                if g >= 2:
                    dve.wait_ge(weighted, columns(g - 1))
                m = n * top
                W = wgt[:, g % 2, 0:m]
                a, c = tent[:, 0, 0:3 * m], tent[:, 1, 0:3 * m]
                spread = [P, 3 * n, top]
                step(nc.vector.tensor_tensor(pos[:, :, 0:n], s2[:, 1, 0:n].unsqueeze(1).to_broadcast([P, 3, n]),
                                             over(tau3[:, :], [P, 3, n]), ALU.mult))
                for q in range(3):
                    last = note(nc.vector.tensor_tensor(
                        a[:, q * m:(q + 1) * m].rearrange("p (t r) -> p t r", t=n),
                        kpos[:, 0:top].unsqueeze(1).to_broadcast([P, n, top]),
                        over(pos[:, q, 0:n], [P, n, top]), ALU.subtract))
                dve.wait_ge(*last)
                step(nc.vector.tensor_scalar(c, a, -1.0, 1.0, ALU.mult, ALU.add))
                step(nc.vector.scalar_tensor_tensor(a, a, 1.0, c, ALU.add, ALU.min))
                by_q = a.rearrange("p (q m) -> p q m", q=3)
                step(nc.vector.scalar_tensor_tensor(by_q, by_q, 0.0, over(share3[:, :], [P, 3, m]),
                                                    ALU.max, ALU.mult))
                note(nc.vector.tensor_reduce(W, a.rearrange("p (q m) -> p m q", q=3), axis=AX.X, op=ALU.add))
                dve.wait_ge(self_in, g + 1)
                last = note(nc.vector.tensor_tensor(body, body, fl[:, 0, 0:(k - 1) * n].unsqueeze(2).to_broadcast(
                    [P, (k - 1) * n, C]), ALU.max))
                layers, _ = network_steps(k, MSP if g < MG else OSP)
                for layer in layers:
                    dve.wait_ge(*last)
                    mins = []
                    for sa, sb_, mn, mx in layer:
                        if mn is not None:
                            mins.append(note(nc.vector.tensor_tensor(
                                G[:, mn, :, 0:C], G[:, sa, :, 0:C], G[:, sb_, :, 0:C], ALU.min)))
                            last = mins[-1]
                        else:
                            mins.append(None)
                    for (sa, sb_, mn, mx), read in zip(layer, mins):
                        if mx is not None:
                            if read:
                                dve.wait_ge(*read)
                            last = note(nc.vector.tensor_tensor(
                                G[:, mx, :, 0:C], G[:, sa, :, 0:C], G[:, sb_, :, 0:C], ALU.max))
                dve.wait_ge(*last)
                note(dve.engine_nop(), sorted_ready)

            def finish(g):
                k, n, q0 = groups[g]
                dve.wait_ge(y_ready, g + 1)
                if 2 <= g < MG + 2:
                    dve.wait_ge(out_done[g % 2], 16 * min(g // 2, MG // 2))
                if g >= MG + 2:
                    dve.wait_ge(scattered[g - 2 - MG], 16 * groups[g - 2][1])
                y = y_ps[:, 0:n, :]
                if g < MG:
                    mk = mask[:, g * T:(g + 1) * T]
                    xs = x_all[:, g * T:(g + 1) * T, :]
                else:
                    mk = rec_of(g, R_MASK, R_MASK + 1).rearrange("p t a -> p (t a)")
                    xs = rec_of(g, R_X, R_X + C)
                step(nc.vector.tensor_tensor(fin2[:, 0:n, :], y, over(mk, [P, n, C]), ALU.mult))
                note(nc.vector.tensor_tensor(fin[:, g % 2, 0:n, :], fin2[:, 0:n, :], xs, ALU.add), fin_ready)

            step(nc.vector.memset(padrow[:, 0:C], BIG))
            note(nc.vector.memset(padrow[:, C:TW], 0.0), pads_made)
            step(nc.vector.memset(padrec[:, 0:LIST + 1], float(PAD)))
            note(nc.vector.memset(padrec[:, LIST + 1:RW], 0.0), pads_made)

            tpos = crow[:, 2, :]
            dve.wait_ge(consts_made, 1)
            for t in range(T):
                clear_diagonal(t)
                tile = adj_ring[:, t // CH, t % CH, :]
                dve.wait_ge(diag_clear, t + 1)
                note(nc.vector.tensor_scalar(tile, tile, 0.0, None, ALU.max), relued_early)
                if t == CH - 1:
                    statistics(0, 1)
            dve.wait_ge(small_in, 16 * 5)
            note(nc.vector.tensor_copy(maskr[:, :], mask8[:, :]), mask_float)
            for b in range(AHEAD):
                if b == 1:
                    statistics(1, B)
                normalise(b)
                list_rows(b)
                dilate(b)
            dve.wait_ge(consts_made, FOLD + 3)
            step(nc.vector.tensor_scalar(tpos, gid[:, :], gid[:, 0:1], 1.0 / P, ALU.subtract, ALU.mult))
            for g in range(len(groups)):
                sort_group(g)
                if g >= 1:
                    finish(g - 1)
                if g + AHEAD < MG:
                    normalise(g + AHEAD)
                    list_rows(g + AHEAD)
                    dilate(g + AHEAD)
                if g + AHEAD == MG - 1:
                    pick_crowded()
                if g == MG - 2:
                    crowded_indices()
            finish(len(groups) - 1)
            with dve.If(general_taken(dve) > 0):
                general_path()

        @block.scalar
        def _(act):
            act.wait_ge(pads_made, 2)
            for b in range(B):
                act.dma_start(tables[b][N:N + 1, :], padrow[:, :]).then_inc(pads_out, 16)
            act.dma_start(table[PAD:PAD + 1, :], padrow[:, :]).then_inc(pads_out, 16)
            act.dma_start(records[PAD:PAD + 1, :], padrec[:, :]).then_inc(pads_out, 16)

            def relu(t):
                c = t // CH
                act.wait_ge(diag_clear, t + 1)
                tile = adj_ring[:, c % NRING, t % CH, :]
                act.activation(tile, tile, ACT.Relu).then_inc(relued, 1)

            def sign(t):
                c = t // CH
                if t < T:
                    act.wait_ge(relued_early, t + 1)
                else:
                    act.wait_ge(relued, t - T + 1)
                if t >= NSIGN:
                    act.wait_ge(keyed_ready, t - NSIGN + 1)
                act.activation(signs[:, t % NSIGN, :], adj_ring[:, c % NRING, t % CH, :], ACT.Sign,
                               accum_out=unlisted[:, t:t + 1]).then_inc(signed, 1)

            def copy_x(b):
                if b >= NREC:
                    act.wait_ge(stored[b % NREC], 32 * (b // NREC))
                else:
                    act.wait_ge(x_in, 16 if b == 0 else 32)
                act.activation(rec[:, b % NREC, :, R_X:R_X + C], x_all[:, b * T:(b + 1) * T, :],
                               ACT.Copy).then_inc(x_copied, 1)

            def first(b):
                act.wait_ge(x_copied, b + 1)
                act.wait_ge(records_ready, b + 1)
                act.dma_start(tables[b][0:N, :].rearrange("(t p) w -> p t w", p=P),
                              rec[:, b % NREC, :, R_H:REC]).then_inc(table_stored[b % NREC], 16)
                act.dma_start(table_t[:, b * T:(b + 1) * T, :],
                              rec[:, b % NREC, :, R_H:REC]).then_inc(stored[b % NREC], 16)
                act.dma_start(records_t[:, b * T:(b + 1) * T, :],
                              rec[:, b % NREC, :, 0:RW]).then_inc(stored[b % NREC], 16)

            def own_value(g):
                k, n, q0 = groups[g]
                if g >= MG:
                    act.wait_ge(crowd_idx, 1)
                if 2 <= g < MG:
                    act.wait_ge(weighted, columns(g - 1))
                act.activation(slots_of(g)[:, k - 1, :, 0:C], rec_of(g, R_H, R_H + C),
                               ACT.Copy).then_inc(self_in, 1)

            def weigh(g, i):
                k, n, q0 = groups[g]
                top = top_rank(k) + 1
                _, where = network_steps(k, MSP if g < MG else OSP)
                for r in range(top):
                    last = act.activation(wsort[:, r * n + i, :], slots_of(g)[:, where[r], i, 0:C], ACT.Copy,
                                          scale=wgt[:, g % 2, i * top + r:i * top + r + 1])
                last.then_inc(weighted, 1)

            def mlp(g):
                k, n, q0 = groups[g]
                cols = n * P
                act.wait_ge(summed, g + 1)
                act.activation(oT[:, 0:cols], oT_ps[:, 0:cols], ACT.Copy).then_inc(sum_out, 1)
                act.wait_ge(hidden, g + 1)
                act.activation(h1[:, 0:cols], h1_ps[:, 0:cols], ACT.Relu, bias=b1s[:, 0:1]).then_inc(hidden_out, 1)

            def store(g):
                if g < MG:
                    act.wait_ge(fin_ready, g + 1)
                    act.dma_start(out_t[:, g * T:(g + 1) * T, :], fin[:, g % 2, :, :]).then_inc(out_done[g % 2], 16)

            t = 0
            for b in range(AHEAD):
                if b < 2:
                    part = var[:, 0:T] if b == 0 else var[:, T:NT]
                    act.wait_ge(var_ready, b + 1)
                    act.activation(part, part, ACT.Sqrt).then_inc(std_ready, 1)
                copy_x(b)
                while t < min((b + 1) * T + T // 2, AHEAD * T):
                    if T <= t + 2 < AHEAD * T:
                        relu(t + 2)
                    sign(t)
                    t += 1
                first(b)
            own_value(0)
            own_value(1)
            act.wait_ge(small_in, 16 * 5)
            for g in range(len(groups)):
                b = g + AHEAD
                n = groups[g][1]
                if b < MG:
                    copy_x(b)
                    for i in range(T):
                        relu(b * T + i)
                    for i in range(T - 1):
                        sign(b * T + i)
                act.wait_ge(sorted_ready, g + 1)
                if g >= 1:
                    act.wait_ge(summed, g)
                for i in range(n):
                    weigh(g, i)
                    if i == 0 and b < MG:
                        sign(b * T + T - 1)
                if g + 2 < len(groups):
                    own_value(g + 2)
                if b < MG:
                    first(b)
                mlp(g)
                if g >= 1:
                    store(g - 1)
            for i in range(2):
                act.wait_ge(out_done[i], 16 * (MG // 2))
            with act.If(general_taken(act) > 0):
                act.wait_ge(all_stored, 1)
                with act.Fori(0, B) as b:
                    act.wait_ge(g_hT_ready, b + 1)
                    act.activation(oT[:, :], h1_ps[0:C, :], ACT.Copy).then_inc(g_hT_out, 1)
                    act.wait_ge(g_hT_stored, 16 * (b + 1))
                    act.wait_ge(g_sum_ready, b + 1)
                    act.activation(oT[:, :], oT_ps, ACT.Copy).then_inc(g_sum_out, 1)
                    act.wait_ge(g_hid_ready, b + 1)
                    act.activation(h1[:, :], h1_ps[:, :], ACT.Relu, bias=b1s[:, 0:1]).then_inc(g_hid_out, 1)

        @block.tensor
        def _(pe):
            def fold_tile(t):
                pe.wait_ge(signed, t + 1)
                if t >= NBANK:
                    pe.wait_ge(tile_taken, t - NBANK + 1)
                ps = key_ps[:, t % NBANK, 0:NF]
                nc.tensor.matmul(ps, ones_h[:, :], key_row[:, :], start=True, stop=False)
                for q in range(FOLD):
                    last = nc.tensor.matmul(ps, eyes[:, q, :], signs[:, t % NSIGN, q * NF:(q + 1) * NF],
                                            start=False, stop=q == FOLD - 1)
                last.then_inc(keyed_ready, 1)

            pe.wait_ge(consts_made, FOLD + 1)
            for t in range(2):
                fold_tile(t)
            for t in range(2, AHEAD * T):
                if t == T:
                    pe.wait_ge(consts_made, FOLD + 3)
                    pe.wait_ge(mask_float, 1)
                    nc.tensor.transpose(m_ps[:, 0:NT], maskr[:, :], ident[0:NT, 0:NT]).then_inc(mask_turned, 1)
                fold_tile(t)
            pe.wait_ge(small_in, 16 * 5)
            for g, (k, n, q0) in enumerate(groups):
                top = top_rank(k) + 1
                b = g + AHEAD
                if b < MG:
                    for i in range(NBANK):
                        fold_tile(b * T + i)
                if g >= 1:
                    pe.wait_ge(hidden_out, g)
                for i in range(n):
                    if b < MG and NBANK + i < T:
                        fold_tile(b * T + NBANK + i)
                    pe.wait_ge(weighted, columns(g) + i + 1)
                    o = oT_ps[:, i * P:(i + 1) * P]
                    nc.tensor.matmul(o, rec_of(g, R_H, R_H + C)[:, i, :], ident[:, :], start=True, stop=False)
                    for r in range(top):
                        last = nc.tensor.matmul(o, wsort[:, r * n + i, :], ident[:, :], start=False,
                                                stop=r == top - 1)
                last.then_inc(summed, 1)
                pe.wait_ge(sum_out, g + 1)
                for a in range(0, n * P, 512):
                    z = min(a + 512, n * P)
                    last = nc.tensor.matmul(h1_ps[:, a:z], w1s[:, :], oT[:, a:z], start=True, stop=True)
                last.then_inc(hidden, 1)
                pe.wait_ge(hidden_out, g + 1)
                if g >= 1:
                    pe.wait_ge(fin_ready, g)
                for i in range(n):
                    nc.tensor.matmul(y_ps[:, i, :], ones1[:, :], b2s[:, :], start=True, stop=False)
                    last = nc.tensor.matmul(y_ps[:, i, :], h1[:, i * P:(i + 1) * P], w2s[:, :],
                                            start=False, stop=True)
                last.then_inc(y_ready, 1)
                if g == PICK:
                    pe.wait_ge(flag_part, 1)
                    nc.tensor.matmul(m_ps[0:1, 0:1], crowd_flag[:, 0:1], crowd_flag[:, 1:2],
                                     start=True, stop=True).then_inc(flag_sum, 1)
            with pe.If(general_taken(pe) > 0):
                pe.wait_ge(all_stored, 1)
                pe.wait_ge(g_const, 3)
                with pe.Fori(0, B) as b:
                    pe.wait_ge(g_h_in, 16 * (b + 1))
                    pe.sem_inc(g_passed, 1)
                    for i in range(T):
                        last = nc.tensor.transpose(h1_ps[0:C, i * P:(i + 1) * P], g_h[:, i, :], ident[:, :])
                    last.then_inc(g_hT_ready, 1)
                    pe.wait_ge(g_gone_ready, b + 1)
                    for i in range(T):
                        pe.wait_ge(g_flip_used, b * T + i + 1)
                        for k in range(T):
                            last = nc.tensor.transpose(flip_ps[:, k * P:(k + 1) * P],
                                                       g_gone[:, k, i * P:(i + 1) * P], g_ident)
                        last.then_inc(g_flip_ready, 1)
                    pe.wait_ge(g_valid_ready, b + 1)
                    for i in range(T):
                        pe.wait_ge(g_turn_out, b * T + i + 1)
                        for k in range(T):
                            last = nc.tensor.transpose(flip_ps[:, k * P:(k + 1) * P],
                                                       g_valid[:, k, i * P:(i + 1) * P], g_ident)
                        last.then_inc(g_turn_ready, 1)
                    pe.wait_ge(g_hT_out, b + 1)
                    pe.sem_inc(g_passed, 1)
                    with pe.Fori(0, C) as c:
                        pe.wait_ge(g_less_ready, b * C + c + 1)
                        for i in range(T):
                            if i >= 2:
                                pe.wait_ge(g_count_used, (b * C + c) * T + i - 1)
                            for half in range(2):
                                for k in range(T):
                                    last = nc.tensor.matmul(
                                        key_ps[:, 2 * (i % 2) + half, :],
                                        g_turned[:, k, i * P:(i + 1) * P], g_less[:, k, half * 512:(half + 1) * 512],
                                        start=k == 0, stop=k == T - 1)
                            last.then_inc(g_count_ready, 1)
                    pe.wait_ge(g_agg_ready, b + 1)
                    for i in range(T):
                        o = oT_ps[:, i * P:(i + 1) * P]
                        nc.tensor.matmul(o, g_h[:, i, :], ident[:, :], start=True, stop=False)
                        last = nc.tensor.matmul(o, g_agg[:, i, :], ident[:, :], start=False, stop=True)
                    last.then_inc(g_sum_ready, 1)
                    pe.wait_ge(g_sum_out, b + 1)
                    for a in range(0, N, 512):
                        last = nc.tensor.matmul(h1_ps[:, a:a + 512], w1s[:, :], oT[:, a:a + 512],
                                                start=True, stop=True)
                    last.then_inc(g_hid_ready, 1)
                    pe.wait_ge(g_hid_out, b + 1)
                    for i in range(T):
                        nc.tensor.matmul(y_ps[:, i, :], ones1[:, :], b2s[:, :], start=True, stop=False)
                        last = nc.tensor.matmul(y_ps[:, i, :], h1[:, i * P:(i + 1) * P], w2s[:, :],
                                                start=False, stop=True)
                    last.then_inc(g_y_ready, 1)


_INS = ['x', 'adj', 'nodemask', 'L0_gnn_W1', 'L0_gnn_b1', 'L0_gnn_W2', 'L0_gnn_b2']


def kernel(**inputs):
    import numpy as _np
    import concourse.bacc as _bacc
    from concourse import mybir as _mybir
    from concourse.bass_utils import run_bass_kernel_spmd as _run

    nc = _bacc.Bacc("TRN2", target_bir_lowering=False, num_devices=1)
    arrays, args = {}, []
    for name in _INS:
        a = _np.ascontiguousarray(inputs[name])
        if a.dtype == _np.bool_:
            a = a.view(_np.uint8)
        arrays[f"in_{name}"] = a
        args.append(nc.dram_tensor(f"in_{name}", a.shape, _mybir.dt.from_np(a.dtype), kind="ExternalInput").ap())
    shape = inputs['x'].shape
    out = nc.dram_tensor("out_0", shape, _mybir.dt.float32, kind="ExternalOutput").ap()
    quantile_gnn(nc, *args, out)
    r = _run(nc, [arrays], core_ids=[0])
    return r.results[0]["out_0"]
```

```python
import concourse.bass as bass
from concourse import mybir
from contextlib import ExitStack

FP32 = mybir.dt.float32
FP16 = mybir.dt.float16
BF16 = mybir.dt.bfloat16
I32 = mybir.dt.int32
ALU = mybir.AluOpType
ACT = mybir.ActivationFunctionType
AX = mybir.AxisListType

NETWORKS = {
    8: [(0, 2), (1, 3), (4, 6), (5, 7), (0, 4), (1, 5), (2, 6), (3, 7), (0, 1), (2, 3), (4, 5), (6, 7),
        (2, 4), (3, 5), (1, 4), (3, 6), (1, 2), (3, 4), (5, 6)],
    10: [(0, 8), (1, 9), (2, 7), (3, 5), (4, 6), (0, 2), (1, 4), (5, 8), (7, 9), (0, 3), (2, 4), (5, 7),
         (6, 9), (0, 1), (3, 6), (8, 9), (1, 5), (2, 3), (4, 8), (6, 7), (1, 2), (3, 5), (4, 6), (7, 8),
         (2, 3), (4, 5), (6, 7), (3, 4), (5, 6)],
    12: [(0, 8), (1, 7), (2, 6), (3, 11), (4, 10), (5, 9), (0, 1), (2, 5), (3, 4), (6, 9), (7, 8), (10, 11),
         (0, 2), (1, 6), (5, 10), (9, 11), (0, 3), (1, 2), (4, 6), (5, 7), (8, 11), (9, 10), (1, 4), (3, 5),
         (6, 8), (7, 10), (1, 3), (2, 5), (6, 9), (8, 10), (2, 3), (4, 5), (6, 7), (8, 9), (4, 6), (5, 7),
         (3, 4), (5, 6), (7, 8)],
}


def odd_even_merge(n):
    net, p = [], 1
    while p < n:
        k = p
        while k >= 1:
            for j in range(k % p, n - k, 2 * k):
                for i in range(min(k, n - j - k)):
                    if (i + j) // (2 * p) == (i + j + k) // (2 * p):
                        net.append((i + j, i + j + k))
            k //= 2
        p *= 2
    return net


NETWORKS[17] = odd_even_merge(17)


def top_rank(slots):
    return -(-3 * (slots - 1) // 4)


def network_steps(slots, spares):
    wanted = set(range(top_rank(slots) + 1))
    kept = []
    wires = min(n for n in NETWORKS if n >= slots)
    for a, b in reversed(NETWORKS[wires]):
        if b < slots and (a in wanted or b in wanted):
            kept.append((a, b, a in wanted, b in wanted))
            wanted |= {a, b}
    kept.reverse()
    at = list(range(slots))
    free = list(range(slots, slots + spares))
    layers = []
    while kept:
        layer, busy, freed, later = [], set(), [], []
        for a, b, low, high in kept:
            if a in busy or b in busy or not free:
                later.append((a, b, low, high))
                busy |= {a, b}
                continue
            busy |= {a, b}
            mn = free.pop(0) if low else None
            layer.append((at[a], at[b], mn, at[b] if high else None))
            if low:
                freed.append(at[a])
                at[a] = mn
        free += freed
        kept = later
        layers.append(layer)
    return layers, at


def quantile_gnn(nc, x, adj, nodemask, W1, b1, W2, b2, out):
    B, N, C = x.shape
    H = W1.shape[1]
    P = 128
    T = N // P
    NT = B * T
    BIG = 1e30
    PAD = B * N
    LIST = 16
    KM = 7
    R_ID, R_CNT, R_KEY, R_MASK = LIST, LIST + 1, LIST + 2, LIST + 3
    R_X = LIST + 4
    R_H = R_X + C
    R_REM = R_H + C
    RW = R_REM
    TW = C + 4
    REC = RW + 4
    TAUS = [(0.25, 0.25), (0.5, 0.5), (0.75, 0.25)]
    CLASSES = [(11, 8, 8), (0, 17, 2), (2, 12, 3), (5, 10, 3), (8, 9, 3)]
    CAPS = [16, 13, 11, 10, 10, 9, 9, 8, 8, 8, 8] + [7] * 8
    NX0 = 14
    NOV = 19
    CH = 2
    NRING = 6
    NCH = NT // CH
    NSIGN = 3
    FOLD = 4
    NF = N // FOLD
    NBANK = 4
    LAG = 2
    AHEAD = 3
    NREC = AHEAD + 1

    MSP, OSP = 4, 3
    MG = B
    order = [*range(MG - 1), MG + 1, MG - 1, MG, *range(MG + 2, MG + len(CLASSES))]
    groups = [(KM, T, None, m) if m < MG else (CLASSES[m - MG][1], CLASSES[m - MG][2], CLASSES[m - MG][0], m)
              for m in order]
    CROWD0 = MG - 1
    PARTS = [(0, 1), (1, AHEAD + 1), (AHEAD + 1, B)]
    PICK = MG - 1 - AHEAD

    x_t = x.rearrange("b (t p) c -> p (b t) c", p=P)
    out_t = out.rearrange("b (t p) c -> p (b t) c", p=P)
    out_rows = out.rearrange("b n c -> (b n) c")
    adj_t = adj.rearrange("b (t p) j -> p (b t) j", p=P)
    tables = [nc.dram_tensor(f"table{b}", [N + 1, TW], FP32, kind="Internal").ap() for b in range(B)]
    table = nc.dram_tensor("table", [PAD + 1, TW], FP32, kind="Internal").ap()
    records = nc.dram_tensor("records", [PAD + 1, RW], FP32, kind="Internal").ap()
    table_t = table[0:PAD, :].rearrange("(t p) w -> p t w", p=P)
    h_turned = nc.dram_tensor("h_turned", [B, C, N], FP32, kind="Internal").ap()
    records_t = records[0:PAD, :].rearrange("(t p) w -> p t w", p=P)

    ctx = ExitStack()
    with ctx:
        def sb(name, shape, dt):
            return ctx.enter_context(nc.sbuf_tensor(name, shape, dt))

        def pb(name, shape):
            return ctx.enter_context(nc.psum_tensor(name, shape, FP32))

        def sem(name):
            return ctx.enter_context(nc.semaphore(name))

        x_all = sb("x_all", [P, NT, C], FP32)
        signs = sb("signs", [P, NSIGN, N], FP16)
        adj_ring = sb("adj_ring", [P, NRING, CH, N], FP32)
        folded2 = sb("folded2", [P, 2, NF], FP32)
        entries = sb("entries", [P, T, LIST], FP32)
        entry_int = sb("entry_int", [P, T, LIST], I32)
        entry_bits = sb("entry_bits", [P, T, LIST], I32)
        entry_key = sb("entry_key", [P, T, LIST], I32)
        one_bit = sb("one_bit", [P, FOLD, T, LIST], I32)
        cand = sb("cand", [P, T, FOLD, LIST], FP32)
        cand2 = sb("cand2", [P, 2, FOLD * LIST], FP32)
        lists = sb("lists", [P, T, LIST], FP32)
        tmpa = sb("tmpa", [P, T, LIST], FP32)
        tmpb = sb("tmpb", [P, T, LIST], FP32)
        tmpc = sb("tmpc", [P, T, LIST], FP32)
        st = sb("st", [P, 2, T], FP32)
        less_mean = sb("less_mean", [P, NT], FP32)
        var = sb("var", [P, NT], FP32)
        scale = sb("scale", [P, NT], FP32)
        shift = sb("shift", [P, NT], FP32)
        xc = sb("xc", [P, T, C], FP32)
        rec = sb("rec", [P, NREC, T, REC], FP32)
        nidx = sb("nidx", [P, NREC, T, KM - 1], I32)
        unlisted = sb("unlisted", [P, NT], FP32)
        degree = sb("degree", [P, NT], FP32)
        gat = sb("gat", [P, 2, KM + MSP, T, TW], FP32)
        wsort = sb("wsort", [P, max(n * (top_rank(k) + 1) for k, n, *_ in groups), C], FP32)
        wmax = max(n * (top_rank(k) + 1) for k, n, *_ in groups)
        wgt = sb("wgt", [P, 2, wmax], FP32)
        fl = sb("fl", [P, 3, max((k - 1) * n for k, n, *_ in groups)], FP32)
        s2 = sb("s2", [P, 2, T], FP32)
        tent = sb("tent", [P, 2, 3 * wmax], FP32)
        pos = sb("pos", [P, 3, T], FP32)
        share3 = sb("share3", [P, 3], FP32)
        key_row = sb("key_row", [1, NF], FP16)
        ones_h = sb("ones_h", [1, P], FP16)
        eyes = sb("eyes", [P, FOLD, P], FP16)
        off_diag = sb("off_diag", [P, P], FP32)
        oT = sb("oT", [C, T * P], FP32)
        h1 = sb("h1", [H, T * P], FP32)
        fin = sb("fin", [P, 2, T, C], FP32)
        fin_crowd = sb("fin_crowd", [P, NOV, C], FP32)
        fin2 = sb("fin2", [P, T, C], FP32)
        ident = sb("ident", [P, P], FP32)
        w1s = sb("w1s", [C, H], FP32)
        b1s = sb("b1s", [H, 1], FP32)
        w2s = sb("w2s", [H, C], FP32)
        b2s = sb("b2s", [1, C], FP32)
        ones1 = sb("ones1", [1, P], FP32)
        mask8 = sb("mask8", [NT, P], mybir.dt.uint8)
        maskr = sb("maskr", [NT, P], FP32)
        mask = sb("mask", [P, NT], FP32)
        kk = sb("kk", [P, LIST], FP32)
        kpos = sb("kpos", [P, LIST], FP32)
        gid = sb("gid", [P, NT], FP32)
        ownkey = sb("ownkey", [P, T], FP32)
        padrow = sb("padrow", [1, TW], FP32)
        padrec = sb("padrec", [1, RW], FP32)
        crow = sb("crow", [P, 3, NT], FP32)
        crowk = sb("crowk", [P, 24], FP32)
        crowi = sb("crowi", [P, 24], I32)
        crowf = sb("crowf", [P, 24], FP32)
        rid = sb("rid", [P, NOV], I32)
        rv = sb("rv", [P, NOV, RW], FP32)
        rvi = sb("rvi", [P, NOV, LIST + 1], I32)

        adj_flat = adj_ring[:, :, :, :].rearrange("p a b n -> p (a b n)")
        _, k, n = CLASSES[0]
        part = gat[:, MG % 2, :, :, :].rearrange("p s t w -> p (s t w)")[:, 0:(k + OSP) * n * TW]
        ov_gat, at = [part.rearrange("p (s t w) -> p s t w", s=k + OSP, t=n)], 0
        for q0, k, n in CLASSES[1:]:
            size = (k + OSP) * n * TW
            ov_gat.append(adj_flat[:, at:at + size].rearrange("p (s t w) -> p s t w", s=k + OSP, t=n))
            at += size
        assert at <= NRING * CH * N

        def ring_part(k, dt, words):
            part = adj_flat[:, k:k + words]
            return part if dt == FP32 else part.bitcast(dt)

        g_adj = ring_part(0, FP32, N)
        g_scan = ring_part(N, FP32, N)
        g_tmp = ring_part(2 * N, FP32, N)
        g_row = ring_part(3 * N, FP32, N)
        g_valid = ring_part(4 * N, BF16, T * N // 2).rearrange("p (t n) -> p t n", t=T)
        g_ones = ring_part(8 * N, BF16, N // 2)
        g_flip = ring_part(9 * N, BF16, N // 2)
        g_ident = ring_part(10 * N, BF16, P // 2)
        g_off = ring_part(10 * N + P, BF16, P // 2)
        g_small = ring_part(11 * N, FP32, 512)
        gat_flat = gat[:, :, :, :, :].rearrange("p a s t w -> p (a s t w)")
        g_gone = gat_flat[:, 0:T * N // 2].bitcast(BF16).rearrange("p (t n) -> p t n", t=T)
        g_less = g_gone
        g_turned = gat_flat[:, T * N // 2:T * N].bitcast(BF16).rearrange("p (t n) -> p t n", t=T)
        g_h = gat_flat[:, T * N:T * N + T * C].rearrange("p (t c) -> p t c", t=T)
        g_agg = gat_flat[:, T * N + T * C:T * N + 2 * T * C].rearrange("p (t c) -> p t c", t=T)

        key_ps = pb("key_ps", [P, NBANK, 512])
        acc_ps = pb("acc_ps", [P, T * P])
        oT_ps = acc_ps[0:C, :]
        h1_ps = acc_ps
        flip_ps = key_ps[:, 0, :].bitcast(BF16)
        count_ps = [key_ps[:, 2 * i:2 * i + 2, :].rearrange("p a n -> p (a n)") for i in range(2)]
        y_ps = pb("y_ps", [P, T, C])
        m_ps = pb("m_ps", [P, 512])
        crowd_flag = sb("crowd_flag", [P, 4], FP32)
        taken = sb("taken", [1, 2], I32)

        def columns(g):
            return sum(n for _, n, *_ in groups[:g])

        def always(m):
            q0, _, n = CLASSES[m - MG]
            return min(n, NX0 - q0)

        def slots_of(g):
            m = order[g]
            return gat[:, m % 2, :, :, :] if m < MG else ov_gat[m - MG]

        def slots_left(g):
            m = order[g]
            if 2 <= m < MG:
                return columns(order.index(m - 2)), True
            return (columns(order.index(MG - 2) + 1), False) if m == MG else (0, False)

        def rec_of(g, a, z):
            k, n, q0, m = groups[g]
            if m < MG:
                return rec[:, m % NREC, :, a:z]
            return rv[:, q0:q0 + n, a:z]

        x_in = sem("x_in")
        small_in = sem("small_in")
        adj_in = [sem(f"adj_in{i}") for i in range(NRING)]
        signed = sem("signed")
        keyed_ready = sem("keyed_ready")
        tile_taken = sem("tile_taken")
        diag_clear = sem("diag_clear")
        relued = sem("relued")
        relued_early = sem("relued_early")
        x_copied = sem("x_copied")
        consts_made = sem("consts_made")
        pool_step = sem("pool_step")
        dve_step = sem("dve_step")
        pads_made = sem("pads_made")
        pads_out = sem("pads_out")
        mask_float = sem("mask_float")
        mask_turned = sem("mask_turned")
        var_ready = sem("var_ready")
        std_ready = sem("std_ready")
        shift_ready = sem("shift_ready")
        h_ready = sem("h_ready")
        count_ready = sem("count_ready")
        tent_step = sem("tent_step")
        tents_ready = sem("tents_ready")
        table_ready = sem("table_ready")
        records_ready = sem("records_ready")
        stored = [sem(f"stored{i}") for i in range(NREC)]
        table_stored = [sem(f"table_stored{i}") for i in range(NREC)]
        self_in = sem("self_in")
        gathered = [sem(f"gathered{i}") for i in range(2)] + [sem(f"gathered_ov{i}") for i in range(len(CLASSES))]
        crowd_ready = sem("crowd_ready")
        recs_gathered = sem("recs_gathered")
        crowd_idx = sem("crowd_idx")
        sorted_ready = sem("sorted_ready")
        weighted = sem("weighted")
        summed = sem("summed")
        sum_out = sem("sum_out")
        hidden = sem("hidden")
        hidden_out = sem("hidden_out")
        y_ready = sem("y_ready")
        fin_ready = sem("fin_ready")
        out_done = [sem(f"out_done{i}") for i in range(2)]
        extra_recs = sem("extra_recs")
        extra_gathered = sem("extra_gathered")
        extra_scattered = sem("extra_scattered")
        extra_recs_in = sem("extra_recs_in")
        extra_cleared = sem("extra_cleared")
        extra_in = sem("extra_in")
        scattered = [sem(f"scattered{i}") for i in range(len(CLASSES))]

        flag_part = sem("flag_part")
        flag_sum = sem("flag_sum")
        flag_ready = sem("flag_ready")
        all_stored = sem("all_stored")
        g_const = sem("g_const")
        g_adj_in = sem("g_adj_in")
        g_adj_used = sem("g_adj_used")
        g_gone_ready = sem("g_gone_ready")
        g_flip_ready = sem("g_flip_ready")
        g_flip_used = sem("g_flip_used")
        g_valid_ready = sem("g_valid_ready")
        g_turn_ready = sem("g_turn_ready")
        g_turn_out = sem("g_turn_out")
        g_h_in = sem("g_h_in")
        g_hT_ready = sem("g_hT_ready")
        g_hT_out = sem("g_hT_out")
        g_hT_stored = sem("g_hT_stored")
        g_row_in = sem("g_row_in")
        g_less_ready = sem("g_less_ready")
        g_count_ready = sem("g_count_ready")
        g_count_used = sem("g_count_used")
        g_chan_done = sem("g_chan_done")
        g_agg_ready = sem("g_agg_ready")
        g_sum_ready = sem("g_sum_ready")
        g_sum_out = sem("g_sum_out")
        g_hid_ready = sem("g_hid_ready")
        g_hid_out = sem("g_hid_out")
        g_y_ready = sem("g_y_ready")
        g_fin_ready = sem("g_fin_ready")
        g_out_done = sem("g_out_done")
        g_passed = sem("g_passed")

        block = ctx.enter_context(nc.Block())

        def general_taken(eng):
            eng.wait_ge(flag_ready, 1)
            return eng.value_load(taken[0:1, 0:1], min_val=0, max_val=1)

        @block.sync
        def _(sp):
            sp.dma_start(x_all[:, 0:T, :], x_t[:, 0:T, :]).then_inc(x_in, 16)
            for c in range(2):
                sp.dma_start(adj_ring[:, c, :, :], adj_t[:, c * CH:(c + 1) * CH, :]).then_inc(adj_in[c], 16)
            sp.dma_start(mask8[:, :], nodemask.rearrange("b (t p) -> (b t) p", p=P)).then_inc(small_in, 16)
            sp.dma_start(w1s[:, :], W1).then_inc(small_in, 16)
            sp.dma_start(b1s[:, :], b1.rearrange("(h a) -> h a", a=1)).then_inc(small_in, 16)
            sp.dma_start(w2s[:, :], W2).then_inc(small_in, 16)
            sp.dma_start(b2s[:, :], b2.rearrange("(a c) -> a c", a=1)).then_inc(small_in, 16)
            for c in range(2, NCH):
                if c == NRING:
                    sp.wait_ge(pads_made, 2)
                    for b in range(B):
                        sp.dma_start(tables[b][N:N + 1, :], padrow[:, :]).then_inc(pads_out, 16)
                    sp.dma_start(table[PAD:PAD + 1, :], padrow[:, :]).then_inc(pads_out, 16)
                    sp.dma_start(records[PAD:PAD + 1, :], padrec[:, :]).then_inc(pads_out, 16)
                if c == 2 * T // CH:
                    sp.wait_ge(x_in, 16)
                    sp.dma_start(x_all[:, T:NT, :], x_t[:, T:NT, :]).then_inc(x_in, 16)
                    sp.wait_ge(table_stored[0], 16)
                if c >= NRING:
                    sp.wait_ge(signed, (c - NRING + 1) * CH)
                sp.dma_start(adj_ring[:, c % NRING, :, :],
                             adj_t[:, c * CH:(c + 1) * CH, :]).then_inc(adj_in[c % NRING], 16)

            with sp.If(general_taken(sp) > 0):
                sp.wait_ge(all_stored, 1)
                with sp.Fori(0, B) as b:
                    sp.dma_start(g_h, records_t[:, bass.ds(b * T, T), R_H:R_H + C]).then_inc(g_h_in, 16)
                    for i in range(T):
                        sp.wait_ge(g_adj_used, b * T + i + 1)
                        sp.dma_start(g_adj, adj_t[:, bass.ds(b * T + i, 1), :].rearrange(
                            "p t n -> p (t n)")).then_inc(g_adj_in, 16)
                    sp.wait_ge(g_hT_out, b + 1)
                    sp.dma_start(h_turned[bass.ds(b, 1), :, :].rearrange("b c n -> c (b n)"),
                                 oT[:, :]).then_inc(g_hT_stored, 16)
                    sp.wait_ge(g_hT_stored, 16 * (b + 1))
                    sp.sem_inc(g_passed, 1)
                    with sp.Fori(0, C) as c:
                        sp.wait_ge(g_chan_done, b * C + c + 1)
                        sp.dma_start(g_row, h_turned[bass.ds(b, 1), bass.ds(c, 1), :].rearrange(
                            "b c n -> (b c) n").partition_broadcast(P)).then_inc(g_row_in, 16)
                    sp.wait_ge(g_fin_ready, b + 1)
                    sp.dma_start(out_t[:, bass.ds(b * T, T), :], fin[:, 0, :, :]).then_inc(g_out_done, 16)
                    sp.wait_ge(g_out_done, 16 * (b + 1))
                    sp.sem_inc(g_passed, 1)

        @block.gpsimd
        def _(pool):
            pool.memset(off_diag[:, :], 1.0).then_inc(pool_step, 1)
            pool.memset(ident[:, :], 0.0).then_inc(pool_step, 1)
            pool.memset(eyes[:, :, :], 0.0).then_inc(pool_step, 1)
            pool.memset(ones_h[:, :], 1.0)
            pool.iota(key_row[:, :], [[-1, NF]], base=NF, channel_multiplier=0,
                      allow_small_or_imprecise_dtypes=True)
            pool.wait_ge(pool_step, 3)
            for m, value in ((off_diag[:, :], 0.0), *((eyes[:, q, :], float(N << q)) for q in range(FOLD)),
                             (ident[:, :], 1.0)):
                pool.affine_select(out=m, in_=m, compare_op=ALU.not_equal, fill=value,
                                   base=0, pattern=[[-1, P]], channel_multiplier=1).then_inc(consts_made, 1)
            pool.iota(kk[:, :], [[1, LIST]], base=1, channel_multiplier=0,
                      allow_small_or_imprecise_dtypes=True)
            pool.iota(kpos[:, :], [[1, LIST]], base=0, channel_multiplier=0,
                      allow_small_or_imprecise_dtypes=True)
            pool.iota(gid[:, :], [[P, NT]], base=0, channel_multiplier=1,
                      allow_small_or_imprecise_dtypes=True)
            pool.iota(ownkey[:, :], [[-P, T]], base=N, channel_multiplier=-1,
                      allow_small_or_imprecise_dtypes=True)
            for q, (_, share) in enumerate(TAUS):
                pool.memset(share3[:, q:q + 1], share)
            pool.memset(ones1[:, :], 1.0).then_inc(consts_made, 1)

            def gather_record(q, done):
                pool.indirect_dma_start(
                    out=rv[:, q, :], out_offset=None, in_=records[:, :],
                    in_offset=bass.IndirectOffsetOnAxis(ap=rid[:, q:q + 1], axis=0),
                    bounds_check=PAD, oob_is_err=False).then_inc(done, 16)

            def gather(g, i0, i1, done):
                k, n, q0, m = groups[g]
                for i in range(i0, i1):
                    left, by_column = slots_left(g)
                    if left or by_column:
                        pool.wait_ge(weighted, left + by_column * (i + 1))
                    for s in range(k - 1 if m < MG else CAPS[q0 + i]):
                        idx = nidx[:, m % NREC, i, s:s + 1] if m < MG else rvi[:, q0 + i, s:s + 1]
                        pool.indirect_dma_start(
                            out=slots_of(g)[:, s, i, :], out_offset=None,
                            in_=tables[m][:, :] if m < MG else table[:, :],
                            in_offset=bass.IndirectOffsetOnAxis(ap=idx, axis=0),
                            bounds_check=N if m < MG else PAD, oob_is_err=False,
                        ).then_inc(done, 16)

            def scatter(g, i0, i1, done):
                k, n, q0, m = groups[g]
                for i in range(i0, i1):
                    pool.indirect_dma_start(
                        out=out_rows, out_offset=bass.IndirectOffsetOnAxis(
                            ap=rvi[:, q0 + i, LIST:LIST + 1], axis=0),
                        in_=fin_crowd[:, q0 + i, :], in_offset=None,
                        bounds_check=PAD - 1, oob_is_err=False).then_inc(done, 16)

            pool.wait_ge(pads_out, 16 * (B + 2))
            for g, (k, n, q0, m) in enumerate(groups):
                if g == CROWD0:
                    pool.wait_ge(crowd_ready, 1)
                    for i in range(NREC):
                        pool.wait_ge(stored[i], 32 * (MG // NREC))
                    for q in range(NX0):
                        gather_record(q, recs_gathered)
                    pool.wait_ge(flag_ready, 1)
                    extra_taken = pool.value_load(taken[0:1, 1:2], min_val=0, max_val=1)
                    with pool.If(extra_taken > 0):
                        for q in range(NX0, NOV):
                            gather_record(q, extra_recs)
                        pool.wait_ge(extra_recs, 16 * (NOV - NX0))
                    pool.engine_nop().then_inc(extra_recs_in, 1)
                    pool.wait_ge(crowd_idx, 1)
                if m < MG:
                    pool.wait_ge(table_stored[m % NREC], 16 * (m // NREC + 1))
                    gather(g, 0, T, gathered[m % 2])
                else:
                    gather(g, 0, always(m), gathered[2 + m - MG])
                    if always(m) < n:
                        pool.wait_ge(extra_cleared, 1)
                        with pool.If(extra_taken > 0):
                            gather(g, always(m), n, extra_gathered)
                            pool.wait_ge(extra_gathered, 16 * (n - always(m)) * (k - 1))
                        pool.engine_nop().then_inc(extra_in, 1)
            for i in range(2):
                pool.wait_ge(out_done[i], 16 * (MG // 2))
            for g, (k, n, q0, m) in enumerate(groups):
                if m < MG:
                    continue
                pool.wait_ge(fin_ready, g + 1)
                scatter(g, 0, always(m), scattered[m - MG])
                if always(m) < n:
                    with pool.If(extra_taken > 0):
                        scatter(g, always(m), n, extra_scattered)
                        pool.wait_ge(extra_scattered, 16 * (n - always(m)))
            for k, n, q0, m in groups:
                if m >= MG:
                    pool.wait_ge(scattered[m - MG], 16 * always(m))
            pool.engine_nop().then_inc(all_stored, 1)

        @block.vector
        def _(dve):
            count = {}

            def note(ins, s=None):
                s = dve_step if s is None else s
                count[id(s)] = count.get(id(s), 0) + 1
                ins.then_inc(s, 1)
                return s, count[id(s)]

            def step(ins, s=None):
                dve.wait_ge(*note(ins, s))

            def row(i):
                return st[:, i, :]

            def over(ap, shape):
                return ap.unsqueeze(2).to_broadcast(shape)

            def statistics(b0, b1):
                dve.wait_ge(x_in, 16 if b0 == 0 else 32)
                for b in range(b0, b1):
                    cut = slice(b * T, (b + 1) * T)
                    xb = x_all[:, cut, :]
                    step(nc.vector.tensor_reduce(less_mean[:, cut], xb, axis=AX.X, op=ALU.add))
                    step(nc.vector.tensor_scalar(less_mean[:, cut], less_mean[:, cut], -1.0 / C, None, ALU.mult))
                    step(nc.vector.tensor_tensor(xc[:, :, :], xb, over(less_mean[:, cut], [P, T, C]), ALU.add))
                    step(nc.vector.tensor_tensor(xc[:, :, :], xc[:, :, :], xc[:, :, :], ALU.mult))
                    step(nc.vector.tensor_reduce(var[:, cut], xc[:, :, :], axis=AX.X, op=ALU.add))
                cut = slice(b0 * T, b1 * T)
                note(nc.vector.tensor_scalar(var[:, cut], var[:, cut], 1.0 / C, 1e-5, ALU.mult, ALU.add), var_ready)

            def scale_and_shift(part):
                cut = slice(PARTS[part][0] * T, PARTS[part][1] * T)
                dve.wait_ge(std_ready, part + 1)
                step(nc.vector.reciprocal(scale[:, cut], var[:, cut]))
                note(nc.vector.tensor_tensor(shift[:, cut], less_mean[:, cut], scale[:, cut], ALU.mult),
                     shift_ready)

            def clear_diagonal(t):
                c, i = t // CH, t % T
                dve.wait_ge(adj_in[c % NRING], 16 * (c // NRING + 1))
                d = adj_ring[:, c % NRING, t % CH, i * P:(i + 1) * P]
                note(nc.vector.tensor_tensor(d, d, off_diag[:, :], ALU.mult), diag_clear)

            def list_rows(b):
                first_lag = LAG if b == 0 else 0
                top8, out8, next8 = {}, {}, {}
                for n in range(first_lag + T + 2):
                    if b == 0 and n == T // 2:
                        dve.wait_ge(small_in, 16 * 5)
                        note(nc.vector.tensor_copy(maskr[:, :], mask8[:, :]), mask_float)
                    if b == 0 and n < T:
                        clear_diagonal(n)
                        tile = adj_ring[:, n // CH, n % CH, :]
                        dve.wait_ge(diag_clear, n + 1)
                        note(nc.vector.tensor_scalar(tile, tile, 0.0, None, ALU.max), relued_early)
                    i = n - first_lag
                    if 0 <= i < T:
                        t = b * T + i
                        dve.wait_ge(keyed_ready, t + 1)
                        top8[i] = note(nc.vector.max(entries[:, i, 0:8], key_ps[:, t % NBANK, 0:NF]))
                    i -= 1
                    if 0 <= i < T:
                        t = b * T + i
                        dve.wait_ge(*top8[i])
                        if i >= 2:
                            dve.wait_ge(*next8[i - 2])
                        out8[i] = note(nc.vector.match_replace(folded2[:, i % 2, :], entries[:, i, 0:8],
                                                               key_ps[:, t % NBANK, 0:NF], 0.0), tile_taken)
                    i -= 1
                    if 0 <= i < T:
                        dve.wait_ge(*out8[i])
                        next8[i] = note(nc.vector.max(entries[:, i, 8:16], folded2[:, i % 2, :]))
                        if 0 < b < B - 1:
                            clear_diagonal(b * T + i + T)
                dve.wait_ge(*next8[T - 1])
                if b == 0:
                    for t in range(T, T + T // 2):
                        clear_diagonal(t)
                step(nc.vector.tensor_copy(entry_int[:, :, :], entries[:, :, :]))
                note(nc.vector.tensor_scalar(entry_key[:, :, :], entry_int[:, :, :], N - 1, None, ALU.bitwise_and))
                step(nc.vector.tensor_scalar(entry_bits[:, :, :], entry_int[:, :, :], N.bit_length() - 1, None,
                                             ALU.logical_shift_right))
                for q in range(FOLD):
                    last = note(nc.vector.tensor_scalar(one_bit[:, q, :, :], entry_bits[:, :, :], q, 1,
                                                        ALU.logical_shift_right, ALU.bitwise_and))
                dve.wait_ge(*last)
                for q in range(FOLD):
                    last = note(nc.vector.scalar_tensor_tensor(
                        cand[:, :, q, :], entry_key[:, :, :], float(N - (q + 1) * NF), one_bit[:, q, :, :],
                        ALU.add, ALU.mult))
                dve.wait_ge(*last)
                for n in range(T + 2):
                    if n < T:
                        top8[n] = note(nc.vector.max(lists[:, n, 0:8], cand[:, n, :, :].rearrange("p q e -> p (q e)")))
                    i = n - 1
                    if 0 <= i < T:
                        dve.wait_ge(*top8[i])
                        if i >= 2:
                            dve.wait_ge(*next8[i - 2])
                        out8[i] = note(nc.vector.match_replace(
                            cand2[:, i % 2, :], lists[:, i, 0:8], cand[:, i, :, :].rearrange("p q e -> p (q e)"), 0.0))
                    i -= 1
                    if 0 <= i < T:
                        dve.wait_ge(*out8[i])
                        next8[i] = note(nc.vector.max(lists[:, i, 8:16], cand2[:, i % 2, :]))
                dve.wait_ge(*next8[T - 1])
            def dilate(b):
                r = rec[:, b % NREC, :, :]
                if b >= NREC:
                    dve.wait_ge(stored[b % NREC], 32 * (b // NREC))
                    dve.wait_ge(table_stored[b % NREC], 16 * (b // NREC))
                else:
                    note(nc.vector.memset(r[:, :, R_REM + 2:R_REM + 4], 0.0))
                deg = degree[:, b * T:(b + 1) * T]
                L, full = lists[:, :, :], [P, T, LIST]
                if b == 0:
                    dve.wait_ge(consts_made, FOLD + 3)
                    dve.wait_ge(mask_turned, 1)
                    step(nc.vector.tensor_copy(mask[:, :], m_ps[:, 0:NT]))
                step(nc.vector.tensor_scalar(tmpa[:, :, :], L, 0.0, None, ALU.is_gt))
                step(nc.vector.tensor_reduce(deg, tmpa[:, :, :], axis=AX.X, op=ALU.add))
                cut = slice(b * T, (b + 1) * T)
                dve.wait_ge(signed, (b + 1) * T)
                note(nc.vector.tensor_tensor(unlisted[:, cut], unlisted[:, cut], deg, ALU.subtract))
                step(nc.vector.tensor_scalar(row(0), deg, 11.0, 6.0, ALU.is_ge, ALU.mult))
                step(nc.vector.scalar_tensor_tensor(row(0), deg, 13.0, row(0), ALU.is_ge, ALU.add))
                step(nc.vector.scalar_tensor_tensor(row(0), deg, 15.0, row(0), ALU.is_ge, ALU.add))
                step(nc.vector.tensor_tensor(row(0), row(0), mask[:, b * T:(b + 1) * T], ALU.mult))
                step(nc.vector.tensor_scalar(row(1), row(0), 2.0, None, ALU.mult))
                places = kk[:, :].unsqueeze(1).to_broadcast(full)
                for n, place in enumerate((row(0), row(1))):
                    step(nc.vector.tensor_tensor(tmpa[:, :, :], places, over(place, full), ALU.is_equal))
                    step(nc.vector.tensor_tensor(tmpb[:, :, :], tmpa[:, :, :], L, ALU.mult))
                    note(nc.vector.tensor_reduce(r[:, :, R_REM + n:R_REM + n + 1], tmpb[:, :, :], axis=AX.X,
                                                 op=ALU.add))
                    step(nc.vector.tensor_tensor(L, L, tmpb[:, :, :], ALU.subtract))
                if b >= NREC:
                    dve.wait_ge(gathered[b % 2], 16 * T * (KM - 1) * ((b - NREC) // 2 + 1))
                note(nc.vector.tensor_scalar(nidx[:, b % NREC, :, :], lists[:, :, 0:KM - 1], -1.0, float(N),
                                             ALU.mult, ALU.add), table_ready)
                step(nc.vector.tensor_scalar(tmpa[:, :, :], L, 0.0, None, ALU.is_gt))
                note(nc.vector.tensor_reduce(r[:, :, R_CNT:R_CNT + 1], tmpa[:, :, :], axis=AX.X, op=ALU.add))
                step(nc.vector.tensor_scalar(tmpb[:, :, :], tmpa[:, :, :], float(b * N + N - PAD), None,
                                             ALU.mult))
                step(nc.vector.scalar_tensor_tensor(tmpc[:, :, :], L, -1.0, tmpb[:, :, :], ALU.mult, ALU.add))
                step(nc.vector.tensor_scalar(r[:, :, 0:LIST], tmpc[:, :, :], float(PAD), None, ALU.add))
                note(nc.vector.tensor_copy(r[:, :, R_ID], gid[:, b * T:(b + 1) * T]))
                note(nc.vector.tensor_copy(r[:, :, R_KEY], ownkey[:, :]))
                note(nc.vector.tensor_copy(r[:, :, R_MASK], mask[:, b * T:(b + 1) * T]), records_ready)

            def pick_crowded():
                k1, k2 = crow[:, 0, :], crow[:, 1, :]
                step(nc.vector.tensor_scalar(k1, degree[:, :], 1.0, float(NT), ALU.add, ALU.mult))
                step(nc.vector.tensor_tensor(k1, k1, tpos, ALU.add))
                step(nc.vector.scalar_tensor_tensor(k1, degree[:, :], float(KM - 1), k1, ALU.is_gt, ALU.mult))
                step(nc.vector.max(crowk[:, 0:8], k1))
                step(nc.vector.match_replace(k2, crowk[:, 0:8], k1, 0.0))
                step(nc.vector.max(crowk[:, 8:16], k2))
                step(nc.vector.match_replace(k1, crowk[:, 8:16], k2, 0.0))
                step(nc.vector.max(crowk[:, 16:24], k1))
                step(nc.vector.tensor_copy(crowi[:, :], crowk[:, :]))
                step(nc.vector.tensor_scalar(crowi[:, :], crowi[:, :], NT - 1, None, ALU.bitwise_and))
                step(nc.vector.tensor_copy(crowf[:, :], crowi[:, :]))
                step(nc.vector.tensor_scalar(crowf[:, :], crowf[:, :], float(P), gid[:, 0:1], ALU.mult, ALU.add))
                step(nc.vector.tensor_scalar(crowf[:, :], crowf[:, :], float(-PAD), None, ALU.add))
                step(nc.vector.scalar_tensor_tensor(crowf[:, :], crowk[:, :], 0.0, crowf[:, :],
                                                    ALU.is_gt, ALU.mult))
                note(nc.vector.memset(rv[:, NX0:NOV, :], 0.0))
                note(nc.vector.tensor_scalar(rid[:, :], crowf[:, 0:NOV], float(PAD), None, ALU.add), crowd_ready)

                f = crowd_flag
                step(nc.vector.tensor_reduce(f[:, 0:1], unlisted[:, :], axis=AX.X, op=ALU.max))
                step(nc.vector.tensor_scalar(f[:, 0:1], f[:, 0:1], 0.0, None, ALU.is_gt))
                step(nc.vector.scalar_tensor_tensor(f[:, 0:1], crowk[:, NOV:NOV + 1], 0.0, f[:, 0:1],
                                                    ALU.is_gt, ALU.max))
                for q in range(NOV):
                    if q == 0 or CAPS[q] < CAPS[q - 1]:
                        step(nc.vector.scalar_tensor_tensor(f[:, 0:1], crowk[:, q:q + 1],
                                                            float((CAPS[q] + 2) * NT), f[:, 0:1],
                                                            ALU.is_ge, ALU.max))
                note(nc.vector.tensor_scalar(f[:, 1:2], crowk[:, NX0:NX0 + 1], 0.0, None, ALU.is_gt))
                note(nc.vector.memset(f[:, 2:3], 1.0), flag_part)

            def general_path():
                dve.wait_ge(all_stored, 1)
                nc.vector.memset(g_ones, 1.0).then_inc(g_const, 1)
                dve.wait_ge(g_const, 1)
                nc.vector.tensor_copy(g_ident, ident[:, :]).then_inc(g_const, 1)
                nc.vector.tensor_scalar(g_off, ident[:, :], -1.0, 1.0, ALU.mult, ALU.add).then_inc(g_const, 1)
                dve.wait_ge(g_const, 3)
                g_k = g_small[:, 64:64 + 6 * T].rearrange("p (t s) -> p t s", t=T)
                g_w = g_small[:, 128:128 + 6 * T].rearrange("p (t s) -> p t s", t=T)
                g_ki = g_small[:, 192:192 + 3 * T].bitcast(I32).rearrange("p (q t) -> p q t", q=3)
                g_kj = g_small[:, 216:216 + 3 * T].bitcast(I32).rearrange("p (q t) -> p q t", q=3)
                g_kf = g_small[:, 240:240 + 3 * T].rearrange("p (q t) -> p q t", q=3)
                g_kg = g_small[:, 264:264 + 3 * T].rearrange("p (q t) -> p q t", q=3)
                g_skip = g_small[:, 288:289]
                g_skipi = g_small[:, 289:290].bitcast(I32)
                g_two = g_small[:, 290:291]
                g_do = g_small[:, 291:292]
                g_cnt = g_small[:, 296:296 + T]
                g_q = g_small[:, 304:310]
                g_q2 = g_small[:, 310:316]

                def sure(ins):
                    dve.drain()

                for free in (g_adj_used, g_chan_done, g_flip_used, g_turn_out):
                    dve.sem_inc(free, 1)
                with dve.Fori(0, B) as b:
                    for i in range(T):
                        dve.wait_ge(g_adj_in, 16 * (b * T + i + 1))
                        nb, gone = g_valid[:, i, :], g_gone[:, i, :]
                        sure(nc.vector.tensor_scalar(nb, g_adj, 0.0, None, ALU.is_gt))
                        dve.sem_inc(g_adj_used, 1)
                        d = g_valid[:, i, i * P:(i + 1) * P]
                        sure(nc.vector.tensor_tensor(d, d, g_off, ALU.mult))
                        sure(nc.vector.tensor_tensor_scan(g_scan, g_ones, nb, 0.0, ALU.mult, ALU.add))
                        m = g_scan[:, N - 1:N]
                        sure(nc.vector.tensor_scalar(g_skipi, m, 1.0, None, ALU.add))
                        sure(nc.vector.tensor_scalar(g_skipi, g_skipi, 1, None, ALU.logical_shift_right))
                        sure(nc.vector.tensor_copy(g_skip, g_skipi))
                        sure(nc.vector.tensor_scalar(g_do, m, 10.0, None, ALU.is_gt))
                        sure(nc.vector.tensor_tensor(g_do, g_do, mask[:, bass.ds(b * T + i, 1)], ALU.mult))
                        sure(nc.vector.tensor_tensor(g_skip, g_skip, g_do, ALU.mult))
                        sure(nc.vector.tensor_scalar(g_two, g_skip, 2.0, None, ALU.mult))
                        sure(nc.vector.tensor_scalar(g_tmp, g_scan, g_skip, None, ALU.is_equal))
                        sure(nc.vector.scalar_tensor_tensor(g_tmp, g_scan, g_two, g_tmp, ALU.is_equal, ALU.add))
                        sure(nc.vector.tensor_tensor(gone, g_tmp, nb, ALU.mult))
                        sure(nc.vector.tensor_tensor(nb, nb, gone, ALU.subtract))
                    dve.sem_inc(g_gone_ready, 1)
                    for i in range(T):
                        v = g_valid[:, i, :]
                        dve.wait_ge(g_flip_ready, b * T + i + 1)
                        sure(nc.vector.tensor_scalar(g_flip, flip_ps, -1.0, 1.0, ALU.mult, ALU.add))
                        dve.sem_inc(g_flip_used, 1)
                        sure(nc.vector.tensor_tensor(v, v, g_flip, ALU.mult))
                        d = g_valid[:, i, i * P:(i + 1) * P]
                        sure(nc.vector.tensor_tensor(d, d, g_ident, ALU.add))
                        sure(nc.vector.tensor_reduce(g_cnt[:, i:i + 1], v, axis=AX.X, op=ALU.add))
                    dve.sem_inc(g_valid_ready, 1)
                    for q in range(3):
                        sure(nc.vector.tensor_scalar(g_ki[:, q, :], g_cnt, -1.0, float(q + 1), ALU.add, ALU.mult))
                    sure(nc.vector.tensor_scalar(g_kj, g_ki, 2, None, ALU.logical_shift_right))
                    sure(nc.vector.tensor_scalar(g_ki, g_ki, 3, None, ALU.bitwise_and))
                    sure(nc.vector.tensor_copy(g_kf, g_kj))
                    sure(nc.vector.tensor_copy(g_kg, g_ki))
                    for q, (tau, share) in enumerate(TAUS):
                        sure(nc.vector.tensor_copy(g_k[:, :, 2 * q], g_kf[:, q, :]))
                        sure(nc.vector.tensor_scalar(g_k[:, :, 2 * q + 1], g_kf[:, q, :], 1.0, None, ALU.add))
                        sure(nc.vector.tensor_scalar(g_w[:, :, 2 * q + 1], g_kg[:, q, :], share / 4, None, ALU.mult))
                        sure(nc.vector.tensor_scalar(g_w[:, :, 2 * q], g_kg[:, q, :], -share / 4, share,
                                                     ALU.mult, ALU.add))
                    for i in range(T):
                        dve.wait_ge(g_turn_ready, b * T + i + 1)
                        sure(nc.vector.tensor_copy(g_turned[:, i, :], flip_ps))
                        dve.sem_inc(g_turn_out, 1)
                    dve.wait_ge(g_h_in, 16 * (b + 1))
                    dve.sem_inc(g_passed, 1)
                    with dve.Fori(0, C) as c:
                        dve.wait_ge(g_row_in, 16 * (b * C + c + 1))
                        for i in range(T):
                            nc.vector.tensor_scalar(g_less[:, i, :], g_row, g_h[:, i, bass.ds(c, 1)], None, ALU.is_gt)
                        dve.drain()
                        dve.sem_inc(g_less_ready, 1)
                        for i in range(T):
                            ps = count_ps[i % 2]
                            dve.wait_ge(g_count_ready, (b * C + c) * T + i + 1)
                            for q in range(6):
                                sure(nc.vector.scalar_tensor_tensor(g_tmp, ps, g_k[:, i, q:q + 1], g_row,
                                                                    ALU.is_le, ALU.mult))
                                sure(nc.vector.tensor_reduce(g_q[:, q:q + 1], g_tmp, axis=AX.X, op=ALU.max))
                            dve.sem_inc(g_count_used, 1)
                            sure(nc.vector.tensor_tensor(g_q2, g_q, g_w[:, i, :], ALU.mult))
                            sure(nc.vector.tensor_reduce(g_agg[:, i, bass.ds(c, 1)], g_q2, axis=AX.X, op=ALU.add))
                        dve.sem_inc(g_chan_done, 1)
                    dve.sem_inc(g_agg_ready, 1)
                    dve.wait_ge(g_y_ready, b + 1)
                    sure(nc.vector.tensor_tensor(fin2[:, :, :], y_ps[:, :, :], over(mask[:, bass.ds(b * T, T)], [P, T, C]),
                                                 ALU.mult))
                    sure(nc.vector.tensor_tensor(fin[:, 0, :, :], fin2[:, :, :], x_all[:, bass.ds(b * T, T), :], ALU.add))
                    dve.sem_inc(g_fin_ready, 1)

            def fill_absent():
                for (q0, k, n), slots in zip(CLASSES[1:], ov_gat[1:]):
                    for i in range(n):
                        if CAPS[q0 + i] < k - 1:
                            note(nc.vector.memset(slots[:, CAPS[q0 + i]:k - 1, i, :], BIG))

            def read_flags():
                dve.wait_ge(flag_sum, 1)
                note(nc.vector.tensor_scalar(taken[:, :], m_ps[0:1, 0:2], 0.0, None, ALU.is_gt), flag_ready)

            def sort_group(g):
                k, n, q0, m = groups[g]
                top = top_rank(k) + 1
                G = slots_of(g)
                if m < MG:
                    dve.wait_ge(gathered[m % 2], 16 * T * (KM - 1) * (m // 2 + 1))
                else:
                    dve.wait_ge(gathered[2 + m - MG], 16 * sum(CAPS[q0:q0 + always(m)]))
                    if always(m) < n:
                        dve.wait_ge(extra_in, 1)
                body = G[:, 0:k - 1, :, 0:C].rearrange("p s t c -> p (s t) c")
                f = [fl[:, i, 0:(k - 1) * n].rearrange("p (s t) -> p s t", s=k - 1) for i in range(3)]
                own = rec_of(g, R_KEY, R_KEY + 1).rearrange("p t a -> p a t").to_broadcast([P, k - 1, n])
                note(nc.vector.tensor_tensor(f[0], G[:, 0:k - 1, :, C], own, ALU.is_equal))
                step(nc.vector.tensor_tensor(f[1], G[:, 0:k - 1, :, C + 1], own, ALU.is_equal))
                step(nc.vector.tensor_tensor(f[2], f[0], f[1], ALU.add))
                note(nc.vector.tensor_scalar(f[0], f[2], BIG, None, ALU.mult))
                step(nc.vector.tensor_reduce(s2[:, 0, 0:n], f[2].rearrange("p s t -> p t s"), axis=AX.X,
                                             op=ALU.add))
                if g >= 1:
                    dve.wait_ge(tents_ready, g)
                step(nc.vector.tensor_tensor(s2[:, 1, 0:n], rec_of(g, R_CNT, R_CNT + 1).rearrange(
                    "p t a -> p (t a)"), s2[:, 0, 0:n], ALU.subtract), count_ready)
                dve.wait_ge(self_in, g + 1)
                last = note(nc.vector.tensor_tensor(body, body, fl[:, 0, 0:(k - 1) * n].unsqueeze(2).to_broadcast(
                    [P, (k - 1) * n, C]), ALU.max))
                layers, _ = network_steps(k, MSP if m < MG else OSP)
                for layer in layers:
                    dve.wait_ge(*last)
                    mins = []
                    for sa, sb_, mn, mx in layer:
                        if mn is not None:
                            mins.append(note(nc.vector.tensor_tensor(
                                G[:, mn, :, 0:C], G[:, sa, :, 0:C], G[:, sb_, :, 0:C], ALU.min)))
                            last = mins[-1]
                        else:
                            mins.append(None)
                    for (sa, sb_, mn, mx), read in zip(layer, mins):
                        if mx is not None:
                            if read:
                                dve.wait_ge(*read)
                            last = note(nc.vector.tensor_tensor(
                                G[:, mx, :, 0:C], G[:, sa, :, 0:C], G[:, sb_, :, 0:C], ALU.max))
                dve.wait_ge(tents_ready, g + 1)
                if g >= 2:
                    dve.wait_ge(weighted, columns(g - 1))
                dve.wait_ge(*last)
                note(nc.vector.tensor_reduce(
                    wgt[:, g % 2, 0:n * top], tent[:, 1, 0:3 * n * top].rearrange("p (q m) -> p m q", q=3),
                    axis=AX.X, op=ALU.add), sorted_ready)

            def finish(g):
                k, n, q0, m = groups[g]
                dve.wait_ge(y_ready, g + 1)
                if 2 <= m < MG:
                    dve.wait_ge(out_done[m % 2], 16 * (m // 2))
                y = y_ps[:, 0:n, :]
                if m < MG:
                    mk = mask[:, m * T:(m + 1) * T]
                    xs = x_all[:, m * T:(m + 1) * T, :]
                    to = fin[:, m % 2, :, :]
                else:
                    mk = rec_of(g, R_MASK, R_MASK + 1).rearrange("p t a -> p (t a)")
                    xs = rec_of(g, R_X, R_X + C)
                    to = fin_crowd[:, q0:q0 + n, :]
                step(nc.vector.tensor_tensor(fin2[:, 0:n, :], y, over(mk, [P, n, C]), ALU.mult))
                note(nc.vector.tensor_tensor(to, fin2[:, 0:n, :], xs, ALU.add), fin_ready)

            step(nc.vector.memset(padrow[:, 0:C], BIG))
            note(nc.vector.memset(padrow[:, C:TW], 0.0), pads_made)
            step(nc.vector.memset(padrec[:, 0:LIST + 1], float(PAD)))
            note(nc.vector.memset(padrec[:, LIST + 1:RW], 0.0), pads_made)

            tpos = crow[:, 2, :]
            dve.wait_ge(consts_made, 1)
            for b in range(AHEAD):
                if b < 2:
                    statistics(*PARTS[b])
                    scale_and_shift(b)
                list_rows(b)
                dilate(b)
                if b == 0:
                    for t in range(T + T // 2, 2 * T):
                        clear_diagonal(t)
            dve.wait_ge(consts_made, FOLD + 3)
            step(nc.vector.tensor_scalar(tpos, gid[:, :], gid[:, 0:1], 1.0 / P, ALU.subtract, ALU.mult))
            for g in range(len(groups)):
                sort_group(g)
                if g == 0:
                    statistics(*PARTS[2])
                if g >= 1:
                    finish(g - 1)
                if g + AHEAD < MG:
                    list_rows(g + AHEAD)
                    dilate(g + AHEAD)
                if g == 0:
                    scale_and_shift(2)
                if g + AHEAD == MG - 1:
                    pick_crowded()
                if g == MG - 3:
                    read_flags()
                    fill_absent()
                if g == CROWD0:
                    dve.wait_ge(weighted, columns(CROWD0))
                    note(nc.vector.memset(ov_gat[0][:, 0:CLASSES[0][1] - 1, always(MG):CLASSES[0][2], :], 0.0), extra_cleared)
            finish(len(groups) - 1)
            with dve.If(general_taken(dve) > 0):
                general_path()

        @block.scalar
        def _(act):
            def relu(t):
                c = t // CH
                act.wait_ge(diag_clear, t + 1)
                tile = adj_ring[:, c % NRING, t % CH, :]
                act.activation(tile, tile, ACT.Relu).then_inc(relued, 1)

            def sign(t):
                c = t // CH
                if t < T:
                    act.wait_ge(relued_early, t + 1)
                else:
                    act.wait_ge(relued, t - T + 1)
                if t >= NSIGN:
                    act.wait_ge(keyed_ready, t - NSIGN + 1)
                act.activation(signs[:, t % NSIGN, :], adj_ring[:, c % NRING, t % CH, :], ACT.Sign,
                               accum_out=unlisted[:, t:t + 1]).then_inc(signed, 1)

            def copy_x(b):
                if b >= NREC:
                    act.wait_ge(stored[b % NREC], 32 * (b // NREC))
                else:
                    act.wait_ge(x_in, 16 if b == 0 else 32)
                act.activation(rec[:, b % NREC, :, R_X:R_X + C], x_all[:, b * T:(b + 1) * T, :],
                               ACT.Copy).then_inc(x_copied, 1)

            def crowded_indices():
                act.wait_ge(recs_gathered, 16 * NX0)
                act.wait_ge(extra_recs_in, 1)
                act.activation(rvi[:, :, :], rv[:, :, 0:LIST + 1], ACT.Copy).then_inc(crowd_idx, 1)

            def normalise(b):
                act.wait_ge(shift_ready, 1 + [a <= b < z for a, z in PARTS].index(True))
                if b >= NREC:
                    act.wait_ge(stored[b % NREC], 32 * (b // NREC))
                    act.wait_ge(table_stored[b % NREC], 16 * (b // NREC))
                    act.wait_ge(summed, b - NREC + 1)
                for i in range(T):
                    t = b * T + i
                    last = act.activation(rec[:, b % NREC, i, R_H:R_H + C], x_all[:, t, :], ACT.Relu,
                                          bias=shift[:, t:t + 1], scale=scale[:, t:t + 1])
                last.then_inc(h_ready, 1)

            def deviations(part):
                v = var[:, PARTS[part][0] * T:PARTS[part][1] * T]
                act.wait_ge(var_ready, part + 1)
                act.activation(v, v, ACT.Sqrt).then_inc(std_ready, 1)

            def tents(g):
                k, n, q0, m = groups[g]
                top = top_rank(k) + 1
                nt = n * top
                act.wait_ge(count_ready, g + 1)
                for q, (tau, _) in enumerate(TAUS):
                    last = act.activation(pos[:, q, 0:n], s2[:, 1, 0:n], ACT.Copy, scale=-tau)
                last.then_inc(tent_step, 1)
                act.wait_ge(tent_step, 2 * g + 1)
                if g >= 1:
                    act.wait_ge(sorted_ready, g)
                for q in range(3):
                    for i in range(n):
                        at = q * nt + i * top
                        last = act.activation(tent[:, 0, at:at + top], kpos[:, 0:top], ACT.Abs,
                                              bias=pos[:, q, i:i + 1])
                last.then_inc(tent_step, 1)
                act.wait_ge(tent_step, 2 * g + 2)
                for q, (_, share) in enumerate(TAUS):
                    last = act.activation(tent[:, 1, q * nt:(q + 1) * nt], tent[:, 0, q * nt:(q + 1) * nt], ACT.Relu,
                                          bias=share3[:, q:q + 1], scale=-share)
                last.then_inc(tents_ready, 1)

            def first(b):
                act.wait_ge(table_ready, b + 1)
                act.wait_ge(h_ready, b + 1)
                act.dma_start(tables[b][0:N, :].rearrange("(t p) w -> p t w", p=P),
                              rec[:, b % NREC, :, R_H:REC]).then_inc(table_stored[b % NREC], 16)
                act.dma_start(table_t[:, b * T:(b + 1) * T, :],
                              rec[:, b % NREC, :, R_H:REC]).then_inc(stored[b % NREC], 16)
                act.wait_ge(x_copied, b + 1)
                act.wait_ge(records_ready, b + 1)
                act.dma_start(records_t[:, b * T:(b + 1) * T, :],
                              rec[:, b % NREC, :, 0:RW]).then_inc(stored[b % NREC], 16)

            def own_value(g):
                k, n, q0, m = groups[g]
                act.wait_ge(h_ready, min(m + 1, B))
                if m >= MG:
                    act.wait_ge(crowd_idx, 1)
                left, by_column = slots_left(g)
                if left or by_column:
                    act.wait_ge(weighted, left + by_column * n)
                act.activation(slots_of(g)[:, k - 1, :, 0:C], rec_of(g, R_H, R_H + C),
                               ACT.Copy).then_inc(self_in, 1)

            def weigh(g, i):
                k, n, q0, m = groups[g]
                top = top_rank(k) + 1
                _, where = network_steps(k, MSP if m < MG else OSP)
                for r in range(top):
                    last = act.activation(wsort[:, r * n + i, :], slots_of(g)[:, where[r], i, 0:C], ACT.Copy,
                                          scale=wgt[:, g % 2, i * top + r:i * top + r + 1])
                last.then_inc(weighted, 1)

            def mlp(g):
                k, n, q0, m = groups[g]
                cols = n * P
                act.wait_ge(summed, g + 1)
                act.activation(oT[:, 0:cols], oT_ps[:, 0:cols], ACT.Copy).then_inc(sum_out, 1)
                act.wait_ge(hidden, g + 1)
                act.activation(h1[:, 0:cols], h1_ps[:, 0:cols], ACT.Relu, bias=b1s[:, 0:1]).then_inc(hidden_out, 1)

            def store(g):
                m = order[g]
                if m < MG:
                    act.wait_ge(fin_ready, g + 1)
                    act.dma_start(out_t[:, m * T:(m + 1) * T, :], fin[:, m % 2, :, :]).then_inc(out_done[m % 2], 16)

            t = 0
            for b in range(AHEAD):
                if b < 2:
                    deviations(b)
                normalise(b)
                copy_x(b)
                while t < min((b + 1) * T + T // 2, AHEAD * T):
                    if t >= T:
                        relu(t)
                    sign(t)
                    t += 1
                first(b)
            own_value(0)
            own_value(1)
            act.wait_ge(small_in, 16 * 5)
            for g in range(len(groups)):
                b = g + AHEAD
                n = groups[g][1]
                if b < MG:
                    for i in range(T // 2 if g >= 1 else 0, T):
                        relu(b * T + i)
                if g == CROWD0 - 1:
                    crowded_indices()
                tents(g)
                if b < MG:
                    for i in range(T - 1):
                        sign(b * T + i)
                    normalise(b)
                    copy_x(b)
                act.wait_ge(sorted_ready, g + 1)
                if g >= 1:
                    act.wait_ge(summed, g)
                for i in range(n):
                    weigh(g, i)
                    if i == 0 and b < MG:
                        sign(b * T + T - 1)
                if g == CROWD0 - 1:
                    own_value(g + 1)
                if g + 2 < len(groups) and g + 2 != CROWD0:
                    own_value(g + 2)
                mlp(g)
                if g == 0:
                    deviations(2)
                if b + 1 < MG:
                    for i in range(T // 2):
                        relu((b + 1) * T + i)
                if b < MG:
                    first(b)
                if g >= 1:
                    store(g - 1)
            for i in range(2):
                act.wait_ge(out_done[i], 16 * (MG // 2))
            with act.If(general_taken(act) > 0):
                act.wait_ge(all_stored, 1)
                with act.Fori(0, B) as b:
                    act.wait_ge(g_hT_ready, b + 1)
                    act.activation(oT[:, :], h1_ps[0:C, :], ACT.Copy).then_inc(g_hT_out, 1)
                    act.wait_ge(g_hT_stored, 16 * (b + 1))
                    act.wait_ge(g_sum_ready, b + 1)
                    act.activation(oT[:, :], oT_ps, ACT.Copy).then_inc(g_sum_out, 1)
                    act.wait_ge(g_hid_ready, b + 1)
                    act.activation(h1[:, :], h1_ps[:, :], ACT.Relu, bias=b1s[:, 0:1]).then_inc(g_hid_out, 1)

        @block.tensor
        def _(pe):
            def fold_tile(t):
                pe.wait_ge(signed, t + 1)
                if t >= NBANK:
                    pe.wait_ge(tile_taken, t - NBANK + 1)
                ps = key_ps[:, t % NBANK, 0:NF]
                nc.tensor.matmul(ps, ones_h[:, :], key_row[:, :], start=True, stop=False)
                for q in range(FOLD):
                    last = nc.tensor.matmul(ps, eyes[:, q, :], signs[:, t % NSIGN, q * NF:(q + 1) * NF],
                                            start=False, stop=q == FOLD - 1)
                last.then_inc(keyed_ready, 1)

            pe.wait_ge(consts_made, FOLD + 1)
            for t in range(2):
                fold_tile(t)
            for t in range(2, AHEAD * T):
                if t == T:
                    pe.wait_ge(consts_made, FOLD + 3)
                    pe.wait_ge(mask_float, 1)
                    nc.tensor.transpose(m_ps[:, 0:NT], maskr[:, :], ident[0:NT, 0:NT]).then_inc(mask_turned, 1)
                fold_tile(t)
            pe.wait_ge(small_in, 16 * 5)
            for g, (k, n, q0, m) in enumerate(groups):
                top = top_rank(k) + 1
                b = g + AHEAD
                if b < MG:
                    for i in range(NBANK):
                        fold_tile(b * T + i)
                if g >= 1:
                    pe.wait_ge(hidden_out, g)
                for i in range(n):
                    if b < MG:
                        for t in range(NBANK + 2 * i, min(NBANK + 2 * i + 2, T)):
                            fold_tile(b * T + t)
                    pe.wait_ge(weighted, columns(g) + i + 1)
                    o = oT_ps[:, i * P:(i + 1) * P]
                    nc.tensor.matmul(o, rec_of(g, R_H, R_H + C)[:, i, :], ident[:, :], start=True, stop=False)
                    for r in range(top):
                        last = nc.tensor.matmul(o, wsort[:, r * n + i, :], ident[:, :], start=False,
                                                stop=r == top - 1)
                last.then_inc(summed, 1)
                pe.wait_ge(sum_out, g + 1)
                for a in range(0, n * P, 512):
                    z = min(a + 512, n * P)
                    last = nc.tensor.matmul(h1_ps[:, a:z], w1s[:, :], oT[:, a:z], start=True, stop=True)
                last.then_inc(hidden, 1)
                pe.wait_ge(hidden_out, g + 1)
                if g >= 1:
                    pe.wait_ge(fin_ready, g)
                for i in range(n):
                    nc.tensor.matmul(y_ps[:, i, :], ones1[:, :], b2s[:, :], start=True, stop=False)
                    last = nc.tensor.matmul(y_ps[:, i, :], h1[:, i * P:(i + 1) * P], w2s[:, :],
                                            start=False, stop=True)
                last.then_inc(y_ready, 1)
                if g == PICK:
                    pe.wait_ge(flag_part, 1)
                    nc.tensor.matmul(m_ps[0:1, 0:2], crowd_flag[:, 2:3], crowd_flag[:, 0:2],
                                     start=True, stop=True).then_inc(flag_sum, 1)
            with pe.If(general_taken(pe) > 0):
                pe.wait_ge(all_stored, 1)
                pe.wait_ge(g_const, 3)
                with pe.Fori(0, B) as b:
                    pe.wait_ge(g_h_in, 16 * (b + 1))
                    pe.sem_inc(g_passed, 1)
                    for i in range(T):
                        last = nc.tensor.transpose(h1_ps[0:C, i * P:(i + 1) * P], g_h[:, i, :], ident[:, :])
                    last.then_inc(g_hT_ready, 1)
                    pe.wait_ge(g_gone_ready, b + 1)
                    for i in range(T):
                        pe.wait_ge(g_flip_used, b * T + i + 1)
                        for k in range(T):
                            last = nc.tensor.transpose(flip_ps[:, k * P:(k + 1) * P],
                                                       g_gone[:, k, i * P:(i + 1) * P], g_ident)
                        last.then_inc(g_flip_ready, 1)
                    pe.wait_ge(g_valid_ready, b + 1)
                    for i in range(T):
                        pe.wait_ge(g_turn_out, b * T + i + 1)
                        for k in range(T):
                            last = nc.tensor.transpose(flip_ps[:, k * P:(k + 1) * P],
                                                       g_valid[:, k, i * P:(i + 1) * P], g_ident)
                        last.then_inc(g_turn_ready, 1)
                    pe.wait_ge(g_hT_out, b + 1)
                    pe.sem_inc(g_passed, 1)
                    with pe.Fori(0, C) as c:
                        pe.wait_ge(g_less_ready, b * C + c + 1)
                        for i in range(T):
                            if i >= 2:
                                pe.wait_ge(g_count_used, (b * C + c) * T + i - 1)
                            for half in range(2):
                                for k in range(T):
                                    last = nc.tensor.matmul(
                                        key_ps[:, 2 * (i % 2) + half, :],
                                        g_turned[:, k, i * P:(i + 1) * P], g_less[:, k, half * 512:(half + 1) * 512],
                                        start=k == 0, stop=k == T - 1)
                            last.then_inc(g_count_ready, 1)
                    pe.wait_ge(g_agg_ready, b + 1)
                    for i in range(T):
                        o = oT_ps[:, i * P:(i + 1) * P]
                        nc.tensor.matmul(o, g_h[:, i, :], ident[:, :], start=True, stop=False)
                        last = nc.tensor.matmul(o, g_agg[:, i, :], ident[:, :], start=False, stop=True)
                    last.then_inc(g_sum_ready, 1)
                    pe.wait_ge(g_sum_out, b + 1)
                    for a in range(0, N, 512):
                        last = nc.tensor.matmul(h1_ps[:, a:a + 512], w1s[:, :], oT[:, a:a + 512],
                                                start=True, stop=True)
                    last.then_inc(g_hid_ready, 1)
                    pe.wait_ge(g_hid_out, b + 1)
                    for i in range(T):
                        nc.tensor.matmul(y_ps[:, i, :], ones1[:, :], b2s[:, :], start=True, stop=False)
                        last = nc.tensor.matmul(y_ps[:, i, :], h1[:, i * P:(i + 1) * P], w2s[:, :],
                                                start=False, stop=True)
                    last.then_inc(g_y_ready, 1)


_INS = ['x', 'adj', 'nodemask', 'L0_gnn_W1', 'L0_gnn_b1', 'L0_gnn_W2', 'L0_gnn_b2']


def kernel(**inputs):
    import numpy as _np
    import concourse.bacc as _bacc
    from concourse import mybir as _mybir
    from concourse.bass_utils import run_bass_kernel_spmd as _run

    nc = _bacc.Bacc("TRN2", target_bir_lowering=False, num_devices=1)
    arrays, args = {}, []
    for name in _INS:
        a = _np.ascontiguousarray(inputs[name])
        if a.dtype == _np.bool_:
            a = a.view(_np.uint8)
        arrays[f"in_{name}"] = a
        args.append(nc.dram_tensor(f"in_{name}", a.shape, _mybir.dt.from_np(a.dtype), kind="ExternalInput").ap())
    shape = inputs['x'].shape
    out = nc.dram_tensor("out_0", shape, _mybir.dt.float32, kind="ExternalOutput").ap()
    quantile_gnn(nc, *args, out)
    r = _run(nc, [arrays], core_ids=[0])
    return r.results[0]["out_0"]
```
